# Optimizing a Trainium2 kernel written in Bass

```python
import numpy as np
import jax
import jax.numpy as jnp

def _softmax(x, axis=-1):
    return jax.nn.softmax(x, axis=axis)

def _gelu(x):
    return jax.nn.gelu(x, approximate=True)

def _silu(x):
    return jax.nn.silu(x)

def _sigmoid(x):
    return jax.nn.sigmoid(x)

def _layernorm(x, axis=-1, eps=1e-05):
    m = jnp.mean(x, axis=axis, keepdims=True)
    v = jnp.var(x, axis=axis, keepdims=True)
    return (x - m) / jnp.sqrt(v + eps)

def _scatter_add(tgt, idx, src, axis=0):
    return tgt.at[idx].add(src)

def _segment_sum(src, seg, n):
    return jax.ops.segment_sum(src, seg, n)
kernel_name = 'mk_sandwich_d1_jaxref_r4_3cd17d'

def setup_inputs(seed: int=0):
    np.random.seed(seed)
    _w = jnp.asarray

    def _L0_attn_setup():
        import math
        import jax, jax.numpy as jnp
        import numpy as np
        B, T, C = (2, 512, 256)
        H, N1, N2, N3 = (16, 6, 4, 6)
        HD = C // H

        def _rotary(T_, hd, dtype):
            inv_freq = 1.0 / 10000.0 ** (jnp.arange(0, hd, 2, dtype=jnp.float32) / hd)
            freqs = jnp.outer(jnp.arange(T_, dtype=jnp.float32), inv_freq)
            return (jnp.cos(freqs)[None, :, None, :].astype(dtype), jnp.sin(freqs)[None, :, None, :].astype(dtype))

        def _apply_rot(x, cos, sin):
            x1, x2 = (x[..., :x.shape[-1] // 2], x[..., x.shape[-1] // 2:])
            return jnp.concatenate([x1 * cos + x2 * sin, -x1 * sin + x2 * cos], axis=-1).astype(x.dtype)

        def _causal_bias(L, S, dtype):
            mask = jnp.triu(jnp.ones((L, S), bool), k=1)
            return jnp.where(mask, jnp.asarray(-jnp.inf, dtype), jnp.asarray(0.0, dtype))

        def _sdpa(q, k, v, scale):
            scores = jnp.einsum('bhtd,bhsd->bhts', q, k) * scale + _causal_bias(q.shape[-2], k.shape[-2], q.dtype)
            return jnp.einsum('bhts,bhsd->bhtd', jax.nn.softmax(scores, axis=-1), v)

        def _hyp_attn(q, k, v, curv):
            eps = 1e-06
            tq = jnp.sqrt(1.0 / curv + jnp.sum(q * q, axis=-1, keepdims=True))
            tk = jnp.sqrt(1.0 / curv + jnp.sum(k * k, axis=-1, keepdims=True))
            inner = jnp.einsum('bhtd,bhsd->bhts', q, k) - tq * jnp.swapaxes(tk, -1, -2)
            arg = jnp.maximum(-curv * inner, 1.0 + 1e-07)
            dis = jnp.sqrt(1.0 / curv) * jnp.arccosh(arg)
            scores = 1.0 / (eps + dis) + _causal_bias(q.shape[-2], k.shape[-2], q.dtype)
            return jnp.einsum('bhts,bhsd->bhtd', jax.nn.softmax(scores, axis=-1), v)
        key = jax.random.key(seed)
        k1, k2, k3 = jax.random.split(key, 3)
        return {'x': jax.random.normal(k1, (B, T, C), jnp.float32), 'qkv_w': jax.random.normal(k2, (3 * C, C), jnp.float32) * C ** (-0.5), 'proj_w': jax.random.normal(k3, (C, C), jnp.float32) * C ** (-0.5), 'proj_b': jnp.zeros((C,), jnp.float32), 'curvature': jnp.ones((1, N2, 1, 1), jnp.float32)}
    _L0_attn_in = _L0_attn_setup()

    def _L0_ffn_setup():
        import jax, jax.numpy as jnp
        import numpy as np
        LN_EPS = 1e-05
        NORM_EPS = 1e-12

        def _layernorm(x, gamma, beta):
            mu = x.mean(axis=-1, keepdims=True)
            var = ((x - mu) ** 2).mean(axis=-1, keepdims=True)
            return (x - mu) * jax.lax.rsqrt(var + LN_EPS) * gamma + beta

        def _l2norm(x, axis):
            n = jnp.sqrt((x ** 2).sum(axis=axis, keepdims=True))
            return x / jnp.maximum(n, NORM_EPS)
        key = jax.random.key(seed)
        ks = jax.random.split(key, 4)
        B, N, D, E, S, H = (64, 64, 256, 16, 16, 64)
        x = jax.random.normal(ks[0], (B, N, D), dtype=jnp.float32)
        mu = jax.random.normal(ks[1], (D, E, S), dtype=jnp.float32) / np.sqrt(D)
        w1 = jax.random.normal(ks[2], (E, D, H), dtype=jnp.float32) * np.sqrt(2.0 / D)
        w2 = jax.random.normal(ks[3], (E, H, D), dtype=jnp.float32) * np.sqrt(2.0 / (H + D))
        return {'x': x, 'ln_gamma': jnp.ones((D,), jnp.float32), 'ln_beta': jnp.zeros((D,), jnp.float32), 'mu': mu, 'scale': jnp.ones((1,), jnp.float32), 'w1': w1, 'b1': jnp.zeros((E, H), jnp.float32), 'w2': w2, 'b2': jnp.zeros((E, D), jnp.float32)}
    _L0_ffn_in = _L0_ffn_setup()
    _d = {'L0_attn_x': _L0_attn_in['x'], 'L0_attn_qkv_w': _L0_attn_in['qkv_w'], 'L0_attn_proj_w': _L0_attn_in['proj_w'], 'L0_attn_proj_b': _L0_attn_in['proj_b'], 'L0_attn_curvature': _L0_attn_in['curvature'], 'L0_ffn_ln_gamma': _L0_ffn_in['ln_gamma'], 'L0_ffn_ln_beta': _L0_ffn_in['ln_beta'], 'L0_ffn_mu': _L0_ffn_in['mu'], 'L0_ffn_scale': _L0_ffn_in['scale'], 'L0_ffn_w1': _L0_ffn_in['w1'], 'L0_ffn_b1': _L0_ffn_in['b1'], 'L0_ffn_w2': _L0_ffn_in['w2'], 'L0_ffn_b2': _L0_ffn_in['b2']}
    _x0 = _d['L0_attn_x']
    _d['L0_attn_x'] = jax.random.normal(jax.random.fold_in(jax.random.key(seed), 1), (4, 2048, 256), dtype=_x0.dtype)
    del _x0
    return _d

def reference(L0_attn_x, L0_attn_qkv_w, L0_attn_proj_w, L0_attn_proj_b, L0_attn_curvature, L0_ffn_ln_gamma, L0_ffn_ln_beta, L0_ffn_mu, L0_ffn_scale, L0_ffn_w1, L0_ffn_b1, L0_ffn_w2, L0_ffn_b2):

    def _L0_attn_ref(x, qkv_w, proj_w, proj_b, curvature):
        import math
        import jax, jax.numpy as jnp
        import numpy as np
        B, T, C = (2, 512, 256)
        H, N1, N2, N3 = (16, 6, 4, 6)
        HD = C // H

        def _rotary(T_, hd, dtype):
            inv_freq = 1.0 / 10000.0 ** (jnp.arange(0, hd, 2, dtype=jnp.float32) / hd)
            freqs = jnp.outer(jnp.arange(T_, dtype=jnp.float32), inv_freq)
            return (jnp.cos(freqs)[None, :, None, :].astype(dtype), jnp.sin(freqs)[None, :, None, :].astype(dtype))

        def _apply_rot(x, cos, sin):
            x1, x2 = (x[..., :x.shape[-1] // 2], x[..., x.shape[-1] // 2:])
            return jnp.concatenate([x1 * cos + x2 * sin, -x1 * sin + x2 * cos], axis=-1).astype(x.dtype)

        def _causal_bias(L, S, dtype):
            mask = jnp.triu(jnp.ones((L, S), bool), k=1)
            return jnp.where(mask, jnp.asarray(-jnp.inf, dtype), jnp.asarray(0.0, dtype))

        def _sdpa(q, k, v, scale):
            scores = jnp.einsum('bhtd,bhsd->bhts', q, k) * scale + _causal_bias(q.shape[-2], k.shape[-2], q.dtype)
            return jnp.einsum('bhts,bhsd->bhtd', jax.nn.softmax(scores, axis=-1), v)

        def _hyp_attn(q, k, v, curv):
            eps = 1e-06
            tq = jnp.sqrt(1.0 / curv + jnp.sum(q * q, axis=-1, keepdims=True))
            tk = jnp.sqrt(1.0 / curv + jnp.sum(k * k, axis=-1, keepdims=True))
            inner = jnp.einsum('bhtd,bhsd->bhts', q, k) - tq * jnp.swapaxes(tk, -1, -2)
            arg = jnp.maximum(-curv * inner, 1.0 + 1e-07)
            dis = jnp.sqrt(1.0 / curv) * jnp.arccosh(arg)
            scores = 1.0 / (eps + dis) + _causal_bias(q.shape[-2], k.shape[-2], q.dtype)
            return jnp.einsum('bhts,bhsd->bhtd', jax.nn.softmax(scores, axis=-1), v)
        Bx, Tx, Cx = x.shape
        qkv = x @ qkv_w.T
        q, k, v = jnp.split(qkv, 3, axis=-1)
        q = q.reshape(Bx, Tx, H, HD)
        k = k.reshape(Bx, Tx, H, HD)
        v = v.reshape(Bx, Tx, H, HD)
        cos, sin = _rotary(Tx, HD, x.dtype)
        q = _apply_rot(q, cos, sin)
        k = _apply_rot(k, cos, sin)
        q, k, v = (jnp.swapaxes(t, 1, 2) for t in (q, k, v))
        outs = []
        outs.append(_sdpa(q[:, :N1], k[:, :N1], v[:, :N1], 1.0 / math.sqrt(HD)))
        outs.append(_hyp_attn(q[:, N1:N1 + N2], k[:, N1:N1 + N2], v[:, N1:N1 + N2], curvature))
        qn = q[:, N1 + N2:] / jnp.maximum(jnp.linalg.norm(q[:, N1 + N2:], axis=-1, keepdims=True), 1e-12)
        kn = k[:, N1 + N2:] / jnp.maximum(jnp.linalg.norm(k[:, N1 + N2:], axis=-1, keepdims=True), 1e-12)
        outs.append(_sdpa(qn, kn, v[:, N1 + N2:], math.sqrt(HD)))
        y = jnp.concatenate(outs, axis=1)
        y = jnp.swapaxes(y, 1, 2).reshape(Bx, Tx, Cx)
        return y @ proj_w.T + proj_b

    def _L0_ffn_ref(x, ln_gamma, ln_beta, mu, scale, w1, b1, w2, b2):
        import jax, jax.numpy as jnp
        import numpy as np
        LN_EPS = 1e-05
        NORM_EPS = 1e-12

        def _layernorm(x, gamma, beta):
            mu = x.mean(axis=-1, keepdims=True)
            var = ((x - mu) ** 2).mean(axis=-1, keepdims=True)
            return (x - mu) * jax.lax.rsqrt(var + LN_EPS) * gamma + beta

        def _l2norm(x, axis):
            n = jnp.sqrt((x ** 2).sum(axis=axis, keepdims=True))
            return x / jnp.maximum(n, NORM_EPS)
        B, N, D = x.shape
        _, E, S = mu.shape
        xn = _layernorm(x, ln_gamma, ln_beta)
        x_unit = _l2norm(xn, axis=-1)
        mu_unit = _l2norm(mu, axis=0)
        logits = jnp.einsum('bnd,des->bnes', x_unit * scale, mu_unit)
        dispatch = jax.nn.softmax(logits, axis=1)
        combine = jax.nn.softmax(logits.reshape(B, N, E * S), axis=-1).reshape(B, N, E, S)
        slot_in = jnp.einsum('bnd,bnes->besd', xn, dispatch)
        h = jax.nn.gelu(jnp.einsum('besd,edh->besh', slot_in, w1) + b1[None, :, None, :], approximate=False)
        slot_out = jnp.einsum('besh,ehd->besd', h, w2) + b2[None, :, None, :]
        out = jnp.einsum('besd,bnes->bnd', slot_out, combine)
        return out
    x = L0_attn_x
    x = x + _layernorm(_L0_attn_ref(_layernorm(x, axis=-1), L0_attn_qkv_w, L0_attn_proj_w, L0_attn_proj_b, L0_attn_curvature), axis=-1)
    x = x + _layernorm(_L0_ffn_ref(_layernorm(x, axis=-1), L0_ffn_ln_gamma, L0_ffn_ln_beta, L0_ffn_mu, L0_ffn_scale, L0_ffn_w1, L0_ffn_b1, L0_ffn_w2, L0_ffn_b2), axis=-1)
    return x

_drawn_inputs = setup_inputs


def setup_inputs(seed=0):
    import zlib

    import numpy as np

    out = dict(_drawn_inputs(seed))
    spreads = {'L0_attn_proj_b': (0.0, 0.1),
     'L0_attn_curvature': (1.0, 0.2),
     'L0_ffn_ln_gamma': (1.0, 0.2),
     'L0_ffn_ln_beta': (0.0, 0.1),
     'L0_ffn_b1': (0.0, 0.1),
     'L0_ffn_b2': (0.0, 0.1)}
    factors = {}
    for name, (base, spread) in spreads.items():
        noise = np.random.default_rng([zlib.crc32(name.encode()), seed]).standard_normal(out[name].shape)
        drawn = base * np.exp(spread * noise) if base else spread * noise
        out[name] = jnp.asarray(drawn.astype(out[name].dtype))
    for name, factor in factors.items():
        out[name] = (out[name] * factor).astype(out[name].dtype)
    return out
```

```python
from contextlib import ExitStack

import concourse.bass as bass
from concourse import mybir

F32 = mybir.dt.float32
BF16 = mybir.dt.bfloat16
ALU = mybir.AluOpType
ACT = mybir.ActivationFunctionType
AX_X = mybir.AxisListType.X

B, T, C = 4, 2048, 256
P = 128
NT = T // P
H, HD = 16, 16
G = 4
NG = H // G
N_STD, N_COS, N_HYP = 6, 6, 4
E, S, HID = 16, 16, 64
SLOTS = E * S
KROWS = 6 * HD + 6
PW = HD + 1
HW3 = 3 * PW
Q_PART = [0, 0, 0, 1, 1, 2]
K_PART = [0, 1, 2, 1, 0, 0]
QT = 512
NQT = T // QT
JB = QT // P
BIG = 1e30
LN_EPS = 1e-5
ARG_MIN = 1.0 + 1.1920929e-07

COS_G, HYP_G = 2, 3
ORDER = [2, 3, 0, 1]
MAX_HEADS = {0: 4, 1: 2, 2: 0, 3: 4}


def units_of_step():
    return [(qt, kb) for qt in range(NQT) for kb in range(JB * (qt + 1))]


UNITS = units_of_step()
NU = len(UNITS)


def max_tasks(g):
    out = []
    for qt in range(NQT):
        for j in range(JB):
            for c in range(qt + 1):
                for h in range(MAX_HEADS[g]):
                    out.append(("chunk", g, qt, j, c, h))
        if g != HYP_G:
            out.append(("split", g, qt))
            for hp in range(MAX_HEADS[g] // 2):
                out.append(("rows", g, qt, hp))
    return out


def plan():
    side = {(s, u): [] for s in range(NG) for u in range(NU)}

    def spread(tasks, s):
        for i, t in enumerate(tasks):
            side[s, i * NU // len(tasks)].append(t)

    spread(max_tasks(HYP_G), 0)
    spread(max_tasks(0) + max_tasks(1), 1)
    return side


FAC = 12
BANKED = ("chunk", "rows", "spread", "untranspose")


def build_constants(nc, ctx, d):
    def sb(name, shape, dt=F32):
        return ctx.enter_context(nc.sbuf_tensor("k_" + name, shape, dt))

    k = {}
    k["ident"] = sb("ident", [P, P])
    k["identb"] = sb("identb", [P, P], BF16)
    k["zero"] = sb("zero", [P, P])
    k["neg_up"] = sb("neg_up", [P, P])
    k["neg_upb"] = sb("neg_upb", [P, P], BF16)
    k["neg_lowb"] = sb("neg_lowb", [P, P], BF16)
    k["pos_upb"] = sb("pos_upb", [P, P], BF16)
    k["eps_ln"] = sb("eps_ln", [P, 1])
    k["eps_dis"] = sb("eps_dis", [P, 1])
    k["m_one"] = sb("m_one", [P, 1])
    k["curv"] = sb("curv", [P, N_HYP])
    k["inv_c"] = sb("inv_c", [P, N_HYP])
    k["root"] = sb("root", [P, N_HYP])
    return k


def block_constants(nc, ctx, k, d):
    const_made = ctx.enter_context(nc.semaphore("const_made"))
    curv_loaded = ctx.enter_context(nc.semaphore("curv_loaded"))
    inv_made = ctx.enter_context(nc.semaphore("inv_made"))
    with nc.Block() as block:
        @block.sync
        def _(sp):
            sp.dma_start(k["curv"][:, :], d["curv"].partition_broadcast(P)).then_inc(curv_loaded, 16)

        @block.gpsimd
        def _(pool):
            g = nc.gpsimd
            n = [0]

            def made(ins):
                n[0] += 1
                ins.then_inc(const_made, 1)
                pool.wait_ge(const_made, n[0])

            g.memset(k["eps_ln"][:, :], LN_EPS)
            g.memset(k["eps_dis"][:, :], 1e-6)
            g.memset(k["m_one"][:, :], -1.0)
            made(g.memset(k["zero"][:, :], 0.0))
            made(g.affine_select(out=k["ident"][:, :], in_=k["zero"][:, :], pattern=[[-1, P]],
                                 compare_op=ALU.not_equal, fill=1.0, base=0, channel_multiplier=1))
            made(g.affine_select(out=k["neg_up"][:, :], in_=k["zero"][:, :], pattern=[[1, P]],
                                 compare_op=ALU.is_ge, fill=-BIG, base=0, channel_multiplier=-1))
            made(g.affine_select(out=k["neg_upb"][:, :], in_=k["zero"][:, :], pattern=[[1, P]],
                                 compare_op=ALU.is_ge, fill=-BIG, base=0, channel_multiplier=-1))
            made(g.affine_select(out=k["pos_upb"][:, :], in_=k["zero"][:, :], pattern=[[1, P]],
                                 compare_op=ALU.is_ge, fill=BIG, base=0, channel_multiplier=-1))
            made(g.affine_select(out=k["neg_lowb"][:, :], in_=k["zero"][:, :], pattern=[[-1, P]],
                                 compare_op=ALU.is_ge, fill=-BIG, base=0, channel_multiplier=1))
            made(g.tensor_copy(k["identb"][:, :], k["ident"][:, :]))

        @block.vector
        def _(dve):
            dve.wait_ge(curv_loaded, 16)
            nc.vector.reciprocal(k["inv_c"][:, :], k["curv"][:, :]).then_inc(inv_made, 1)

        @block.scalar
        def _(act):
            act.wait_ge(inv_made, 1)
            nc.scalar.activation(k["root"][:, :], k["inv_c"][:, :], ACT.Sqrt)


def block_project(nc, k, d):
    ctx = ExitStack()
    with ctx:
        def sb(name, shape, dt=F32):
            return ctx.enter_context(nc.sbuf_tensor("a_" + name, shape, dt))

        def ps(name, dt=F32):
            return ctx.enter_context(nc.psum_tensor("a_" + name, [P, 2048 // (4 if dt == F32 else 2)], dt))

        def sem(name):
            return ctx.enter_context(nc.semaphore("a_" + name))

        w = sb("w", [P, 2, 3 * C])
        cos = sb("cos", [P, NT, 8])
        sin = sb("sin", [P, NT, 8])
        X = sb("X", [P, NT, C])
        xn = sb("xn", [P, 2, C])
        xT = sb("xT", [P, 2, 2, P])
        T1 = sb("T1", [P, 2, 64, 8])
        T2 = sb("T2", [P, 2, 64, 8])
        QK = sb("QK", [P, NT, 2 * C])
        SQ = sb("SQ", [P, 2 * NT, 10 * HD])
        V = sb("V", [P, NG, NT, G, 32])
        F = sb("F", [P, NT, 2, H])
        N2 = sb("N2", [P, 2 * NT, 10])
        RN = sb("RN", [P, NT, 2, N_COS])
        HN = sb("HN", [P, NT, 2, N_HYP])
        HT = sb("HT", [P, NT, 2, N_HYP])
        AU = sb("AU", [P, NT, 2, N_HYP])
        AR = sb("AR", [P, NT, 2, N_HYP])
        AP3 = sb("AP3", [P, NT, 2 * N_HYP, 3], BF16)
        stats = sb("stats", [P, NT, 6])
        st = sb("st", [P, 6, NT])
        QKS = sb("QKS", [P, 2, 2 * H, HD])
        R = sb("R", [P, 2, 2 * H, HD])
        ST = sb("ST", [P, 2, 2 * H, HW3], BF16)
        TS = sb("TS", [P, 2, H // 2, T], BF16)

        xt_bank = [ps(f"xt{u}") for u in range(2)]
        qk_bank = [ps(f"qk{u}") for u in range(2)]
        v_bank = [ps(f"v{u}") for u in range(2)]
        tq_bank = [xt_bank[u][:, :].bitcast(BF16) for u in range(2)]
        tk_bank = [qk_bank[u][:, :].bitcast(BF16) for u in range(2)]

        w_loaded, x_loaded = sem("w_loaded"), sem("x_loaded")
        filled = sem("filled")
        x_free, bs_done, var_ready, std_ready, rstd_ready = map(
            sem, ["x_free", "bs_done", "var_ready", "std_ready", "rstd_ready"])
        xn_ready, xt_psum, xt_ready, qkv_done, rot_done, qk_ready, v_ready = map(
            sem, ["xn_ready", "xt_psum", "xt_ready", "qkv_done", "rot_done", "qk_ready", "v_ready"])
        nsq_ready, roots_ready, fac_step = map(sem, ["nsq_ready", "roots_ready", "fac_step"])
        sc_done, hi_done, r_done, mid_done, lo_done, aug_done, tp_done, evq_done, evk_done = map(
            sem, ["sc_done", "hi_done", "r_done", "mid_done", "lo_done", "aug_done", "tp_done", "evq_done",
                  "evk_done"])
        v_stored, parts_stored = sem("v_stored"), sem("parts_stored")
        NW = 3

        with nc.Block() as block:
            @block.sync
            def _(sp):
                sp.dma_start(w[:, :, :], d["wqkv"].rearrange("(k p) n -> p k n", p=P)).then_inc(w_loaded, 16)
                sp.dma_start(cos[:, :, :], d["cos"].rearrange("(n p) f -> p n f", p=P)).then_inc(w_loaded, 16)
                sp.dma_start(sin[:, :, :], d["sin"].rearrange("(n p) f -> p n f", p=P)).then_inc(w_loaded, 16)
                with sp.Fori(0, B) as b:
                    sp.wait_ge(x_free, b * NT + 1)
                    sp.dma_start(X[:, :, :], d["x"][bass.ds(b, 1), :, :].rearrange(
                        "o (n p) c -> p (o n) c", p=P)).then_inc(x_loaded, 16)
                    sp.wait_ge(v_ready, b * NT + NT + 2)
                    sp.dma_start(d["v_dram"][bass.ds(b, 1), :, :, :, :].rearrange("o g p n x -> p (o g) n x"),
                                 V[:, :, :, :, :].rearrange("p g n h x -> p g n (h x)")).then_inc(v_stored, 16)
                    sp.wait_ge(evq_done, b * NT + NT + 2)
                    sp.wait_ge(evk_done, b * NT + NT + 2)
                    for qk in range(2):
                        sp.dma_start(d["parts"][bass.ds(b, 1), qk, :, :, :].rearrange("o a r t -> r (o a) t"),
                                     TS[0:2 * HW3, qk, :, :]).then_inc(parts_stored, 16)
                sp.wait_ge(v_stored, 16 * B + 16)
                sp.wait_ge(parts_stored, 32 * B + 32)

            @block.gpsimd
            def _(pool):
                g = nc.gpsimd
                g.memset(V[:, :, :, :, :], 0.0).then_inc(filled, 1)
                pool.wait_ge(filled, 1)
                g.memset(V[:, :, :, :, 16:17], 1.0).then_inc(filled, 1)
                g.memset(ST[:, :, :, :], 1.0).then_inc(filled, 1)
                pool.wait_ge(filled, 3)
                stv = ST[:, :, :, :].rearrange("p u h (a w) -> p u h a w", w=PW)
                for u in range(2):
                    g.memset(stv[:, u, 0:H, :, HD], 0.0).then_inc(filled, 1)
                g.memset(F[:, :, :, :], 1.0).then_inc(filled, 1)
                pool.wait_ge(filled, 6)
                g.memset(F[:, :, 0, 0:N_STD], HD ** -0.5).then_inc(filled, 1)
                pool.wait_ge(filled, 7)
                for h in range(N_HYP):
                    g.tensor_scalar(F[:, :, 1, 12 + h], F[:, :, 1, 12 + h], k["curv"][:, h:h + 1], -1.0,
                                    ALU.mult, ALU.mult).then_inc(filled, 1)
                with pool.Fori(0, B) as b:
                    with pool.Fori(0, NT // 2) as m:
                        for u in range(2):
                            i = b * NT + m * 2 + u
                            pool.wait_ge(rot_done, i + 3)
                            n = m * 2 + u
                            qk = QK[:, bass.ds(n, 1), :].rearrange("p o (a s f) -> p (o a) s f", s=2, f=8)
                            t1 = T1[:, u, :, :].rearrange("p (a s) f -> p a s f", s=2)
                            t2 = T2[:, u, :, :].rearrange("p (a s) f -> p a s f", s=2)
                            g.tensor_tensor(qk[:, :, 0, :], t1[:, :, 0, :], t2[:, :, 1, :], ALU.add)
                            g.tensor_tensor(qk[:, :, 1, :], t1[:, :, 1, :], t2[:, :, 0, :],
                                            ALU.subtract).then_inc(qk_ready, 1)
                    with pool.Fori(0, NT // 2) as m:
                        pool.wait_ge(fac_step, (b + 1) * FAC)
                        for u in range(2):
                            i = b * NT + m * 2 + u
                            n = m * 2 + u
                            pool.wait_ge(tp_done, i + 1)
                            for qk_ in range(2):
                                o = ST[:, u, :, :].rearrange("p (q h) (a w) -> p q h a w", q=2, w=PW)
                                ins = g.tensor_copy(o[:, qk_, 12:16, :, HD],
                                                    AP3[:, bass.ds(n, 1), qk_ * 4:qk_ * 4 + 4, :].rearrange(
                                                        "p o h a -> p (o h) a"))
                            ins.then_inc(aug_done, 1)

            @block.vector
            def _(dve):
                v = nc.vector
                dve.sem_inc(rot_done, 2)
                dve.sem_inc(evq_done, 2)
                dve.wait_ge(w_loaded, 16 * NW)
                dve.wait_ge(filled, 11)
                with dve.Fori(0, B) as b:
                    with dve.Fori(0, NT) as n:
                        dve.wait_ge(x_loaded, b * 16 + 16)
                        v.bn_stats(stats[:, bass.ds(n, 1), :].rearrange("p o s -> p (o s)"),
                                   X[:, bass.ds(n, 1), :].rearrange("p o c -> p (o c)")).then_inc(bs_done, 1)
                    dve.wait_ge(bs_done, b * NT + NT)
                    layer_norm_stats(nc, dve, stats, st, b, var_ready, std_ready, rstd_ready)
                    with dve.Fori(0, NT // 2) as m:
                        for u in range(2):
                            i = b * NT + m * 2 + u
                            n = m * 2 + u
                            dve.wait_ge(qkv_done, i + 3)
                            dve.wait_ge(qk_ready, i + 1)
                            src = qk_bank[u][:, :].rearrange("p (a f) -> p a f", f=8)
                            v.tensor_tensor(T1[:, u, :, :], src,
                                            cos[:, bass.ds(n, 1), :].to_broadcast([P, 64, 8]), ALU.mult)
                            v.tensor_tensor(T2[:, u, :, :], src,
                                            sin[:, bass.ds(n, 1), :].to_broadcast([P, 64, 8]),
                                            ALU.mult).then_inc(rot_done, 1)
                    dve.wait_ge(qk_ready, b * NT + NT + 2)
                    steps = [0]

                    def step(ins):
                        steps[0] += 1
                        ins.then_inc(fac_step, 1)

                    def wait_steps():
                        dve.wait_ge(fac_step, b * FAC + steps[0])

                    norm_of = QK[:, :, :].rearrange("p n (q c) -> p (n q) c", q=2)[:, :, N_STD * HD:C]
                    step(v.tensor_tensor(SQ[:, :, :], norm_of, norm_of, ALU.mult))
                    wait_steps()
                    step(v.tensor_reduce(N2[:, :, :], SQ[:, :, :].rearrange("p m (h e) -> p m h e", e=HD),
                                         AX_X, ALU.add))
                    wait_steps()
                    n2 = N2[:, :, :].rearrange("p (n q) h -> p n q h", q=2)
                    step(v.tensor_tensor(HN[:, :, :, :].rearrange("p n q h -> p (n q) h"), N2[:, :, 6:10],
                                         k["inv_c"][:, :].unsqueeze(1).to_broadcast([P, 2 * NT, N_HYP]), ALU.add))
                    dve.wait_ge(roots_ready, b + 1)
                    step(v.tensor_scalar(RN[:, :, :, :], RN[:, :, :, :], 1e-12, None, ALU.max))
                    step(v.tensor_copy(AU[:, :, 0, :], HT[:, :, 0, :]))
                    step(v.tensor_tensor(AU[:, :, 1, :], HT[:, :, 1, :],
                                         k["curv"][:, :].unsqueeze(1).to_broadcast([P, NT, N_HYP]), ALU.mult))
                    wait_steps()
                    step(v.reciprocal(F[:, :, :, 6:12], RN[:, :, :, :]))
                    aug = AU[:, :, :, :].rearrange("p n q h -> p n (q h)")
                    rest = AR[:, :, :, :].rearrange("p n q h -> p n (q h)")
                    step(v.tensor_copy(AP3[:, :, :, 0], aug))
                    wait_steps()
                    step(v.tensor_scalar(F[:, :, 0, 6:12], F[:, :, 0, 6:12], HD ** 0.5, None, ALU.mult))
                    step(v.tensor_tensor(rest, aug, AP3[:, :, :, 0], ALU.subtract))
                    wait_steps()
                    step(v.tensor_copy(AP3[:, :, :, 1], rest))
                    wait_steps()
                    step(v.tensor_tensor(AP3[:, :, :, 2], rest, AP3[:, :, :, 1], ALU.subtract))
                    assert steps[0] == FAC
                    with dve.Fori(0, NT // 2) as m:
                        wait_steps()
                        dve.wait_ge(parts_stored, b * 32 + 32)
                        stv = [ST[:, u, :, :].rearrange("p h (a w) -> p h a w", w=PW) for u in range(2)]
                        for u in range(2):
                            i = b * NT + m * 2 + u
                            n = m * 2 + u
                            dve.wait_ge(lo_done, i + 1)
                            dve.wait_ge(hi_done, i + 1)
                            v.tensor_tensor(QKS[:, u, :, :],
                                            QK[:, bass.ds(n, 1), :].rearrange("p o (h e) -> p (o h) e", e=HD),
                                            F[:, bass.ds(n, 1), :, :].rearrange("p o q h -> p (o q h)").unsqueeze(
                                                2).to_broadcast([P, 2 * H, HD]), ALU.mult).then_inc(sc_done, 1)
                        for u in range(2):
                            i = b * NT + m * 2 + u
                            dve.wait_ge(hi_done, i + 3)
                            dve.wait_ge(mid_done, i + 1)
                            v.tensor_tensor(R[:, u, :, :], QKS[:, u, :, :], stv[u][:, :, 0, 0:HD],
                                            ALU.subtract).then_inc(r_done, 1)
                        for u in range(2):
                            i = b * NT + m * 2 + u
                            dve.wait_ge(mid_done, i + 3)
                            v.tensor_tensor(stv[u][:, :, 2, 0:HD], R[:, u, :, :], stv[u][:, :, 1, 0:HD],
                                            ALU.subtract).then_inc(lo_done, 1)
                        for u in range(2):
                            i = b * NT + m * 2 + u
                            dve.wait_ge(tp_done, i + 3)
                            v.tensor_copy(TS[0:2 * HW3, 0, :, bass.ds(m * 2 * P + u * P, P)],
                                          tq_bank[u][0:2 * HW3, :].rearrange("p (a t) -> p a t", t=P)
                                          ).then_inc(evq_done, 1)

            @block.scalar
            def _(act):
                a = nc.scalar
                act.sem_inc(x_free, 1)
                act.sem_inc(xt_ready, 2)
                act.sem_inc(v_ready, 2)
                act.sem_inc(hi_done, 2)
                act.sem_inc(mid_done, 2)
                act.sem_inc(evk_done, 2)
                act.sem_inc(v_stored, 16)
                act.sem_inc(parts_stored, 32)
                act.wait_ge(filled, 11)
                with act.Fori(0, B) as b:
                    act.wait_ge(var_ready, b * VAR + VAR)
                    a.activation(st[:, 4, :], st[:, 3, :], ACT.Sqrt, bias=k["eps_ln"][:, :],
                                 scale=1.0 / C).then_inc(std_ready, 1)
                    act.wait_ge(rstd_ready, b * 2 + 2)
                    act.wait_ge(v_stored, b * 16 + 16)
                    with act.Fori(0, NT // 2) as m:
                        for u in range(2):
                            i = b * NT + m * 2 + u
                            n = m * 2 + u
                            act.wait_ge(xt_psum, i + 1)
                            a.activation(xn[:, u, :], X[:, bass.ds(n, 1), :].rearrange("p o c -> p (o c)"),
                                         ACT.Identity, bias=st[:, 0, bass.ds(n, 1)],
                                         scale=st[:, 5, bass.ds(n, 1)]).then_inc(xn_ready, 1)
                        for u in range(2):
                            i = b * NT + m * 2 + u
                            act.wait_ge(xt_psum, i + 3)
                            act.wait_ge(qkv_done, i + 1)
                            a.copy(xT[:, u, :, :].rearrange("p k t -> p (k t)"),
                                   xt_bank[u][:, 0:C]).then_inc(xt_ready, 1)
                        for u in range(2):
                            i = b * NT + m * 2 + u
                            n = m * 2 + u
                            act.wait_ge(qkv_done, i + 3)
                            a.copy(V[:, :, bass.ds(n, 1), :, 0:HD].rearrange("p g o h e -> p g (o h) e"),
                                   v_bank[u][:, 0:C].rearrange("p (g h e) -> p g h e", g=NG, e=HD)).then_inc(v_ready, 1)
                    act.wait_ge(xn_ready, b * NT + NT)
                    act.sem_inc(x_free, NT)
                    act.wait_ge(fac_step, b * FAC + 3)
                    a.activation(RN[:, :, :, :], N2[:, :, 0:6].rearrange("p (n q) h -> p n q h", q=2), ACT.Sqrt)
                    a.activation(HT[:, :, :, :], HN[:, :, :, :], ACT.Sqrt).then_inc(roots_ready, 1)
                    act.wait_ge(parts_stored, b * 32 + 32)
                    stv = [ST[:, u, :, :].rearrange("p h (a w) -> p h a w", w=PW) for u in range(2)]
                    with act.Fori(0, NT // 2) as m:
                        for u in range(2):
                            i = b * NT + m * 2 + u
                            act.wait_ge(sc_done, i + 1)
                            act.wait_ge(tp_done, i + 1)
                            a.copy(stv[u][:, :, 0, 0:HD], QKS[:, u, :, :]).then_inc(hi_done, 1)
                        for u in range(2):
                            i = b * NT + m * 2 + u
                            act.wait_ge(r_done, i + 1)
                            a.copy(stv[u][:, :, 1, 0:HD], R[:, u, :, :]).then_inc(mid_done, 1)
                        for u in range(2):
                            i = b * NT + m * 2 + u
                            act.wait_ge(tp_done, i + 3)
                            a.copy(TS[0:2 * HW3, 1, :, bass.ds(m * 2 * P + u * P, P)],
                                   tk_bank[u][0:2 * HW3, :].rearrange("p (a t) -> p a t", t=P)
                                   ).then_inc(evk_done, 1)

            @block.tensor
            def _(pe):
                t = nc.tensor
                pe.sem_inc(xt_psum, 2)
                pe.sem_inc(qkv_done, 2)
                pe.sem_inc(qk_ready, 2)
                pe.sem_inc(lo_done, 2)
                pe.sem_inc(tp_done, 2)
                pe.wait_ge(w_loaded, 16 * NW)
                with pe.Fori(0, B) as b:
                    with pe.Fori(0, NT // 2) as m:
                        pe.wait_ge(evq_done, b * NT + 2)
                        pe.wait_ge(evk_done, b * NT + 2)
                        for u in range(2):
                            i = b * NT + m * 2 + u
                            pe.wait_ge(xn_ready, i + 1)
                            pe.wait_ge(xt_ready, i + 1)
                            for c in range(2):
                                ins = t.transpose(xt_bank[u][:, c * P:(c + 1) * P], xn[:, u, c * P:(c + 1) * P],
                                                  k["ident"][:, :])
                            ins.then_inc(xt_psum, 1)
                        for u in range(2):
                            i = b * NT + m * 2 + u
                            pe.wait_ge(xt_ready, i + 3)
                            pe.wait_ge(rot_done, i + 1)
                            pe.wait_ge(v_ready, i + 1)
                            for c in range(2):
                                t.matmul(qk_bank[u][:, :], xT[:, u, c, :], w[:, c, 0:2 * C], start=(c == 0),
                                         stop=(c == 1))
                            for c in range(2):
                                ins = t.matmul(v_bank[u][:, 0:C], xT[:, u, c, :], w[:, c, 2 * C:3 * C],
                                               start=(c == 0), stop=(c == 1))
                            ins.then_inc(qkv_done, 1)
                    with pe.Fori(0, NT // 2) as m:
                        pe.wait_ge(xt_ready, b * NT + NT + 2)
                        pe.wait_ge(rot_done, b * NT + NT + 2)
                        for u in range(2):
                            i = b * NT + m * 2 + u
                            pe.wait_ge(lo_done, i + 3)
                            pe.wait_ge(hi_done, i + 3)
                            pe.wait_ge(mid_done, i + 3)
                            pe.wait_ge(aug_done, i + 1)
                            pe.wait_ge(evq_done, i + 1)
                            pe.wait_ge(evk_done, i + 1)
                            st_ = ST[:, u, :, :].rearrange("p (a x) w -> p a (x w)", x=2)
                            for qk in range(2):
                                bank = (tq_bank, tk_bank)[qk][u]
                                for a in range(H // 2):
                                    ins = t.transpose(bank[0:2 * HW3, a * P:(a + 1) * P], st_[:, 8 * qk + a, :],
                                                      k["identb"][:, :])
                            ins.then_inc(tp_done, 1)


VAR = 5


def layer_norm_stats(nc, dve, stats, st, b, var_ready, std_ready, rstd_ready):
    v = nc.vector
    pick = stats[:, :, :].rearrange("p n s -> p s n")
    v.tensor_tensor(st[:, 0, :], pick[:, 1, :], pick[:, 4, :], ALU.add).then_inc(var_ready, 1)
    v.tensor_tensor(st[:, 1, :], pick[:, 1, :], pick[:, 4, :], ALU.subtract).then_inc(var_ready, 1)
    v.tensor_tensor(st[:, 2, :], pick[:, 2, :], pick[:, 5, :], ALU.add).then_inc(var_ready, 1)
    dve.wait_ge(var_ready, b * VAR + 3)
    v.tensor_tensor(st[:, 4, :], st[:, 1, :], st[:, 1, :], ALU.mult).then_inc(var_ready, 1)
    dve.wait_ge(var_ready, b * VAR + 4)
    v.scalar_tensor_tensor(out=st[:, 3, :], in0=st[:, 4, :], scalar=C / 4.0, in1=st[:, 2, :], op0=ALU.mult,
                           op1=ALU.add).then_inc(var_ready, 1)
    dve.wait_ge(std_ready, b + 1)
    v.reciprocal(st[:, 5, :], st[:, 4, :]).then_inc(rstd_ready, 1)
    dve.wait_ge(rstd_ready, b * 2 + 1)
    v.scalar_tensor_tensor(out=st[:, 0, :], in0=st[:, 0, :], scalar=-0.5, in1=st[:, 5, :], op0=ALU.mult,
                           op1=ALU.mult).then_inc(rstd_ready, 1)


NS = NG * NU
NP = 2 * NS
NTILE = NG * NQT
MSPLIT = 5
HYP_DVE, HYP_ACT = 5, 5


def block_attend(nc, k, d):
    side = plan()
    step_of = {g: s for s, g in enumerate(ORDER)}

    units = [(s, ORDER[s], u, qt, kb) for s in range(NG) for u, (qt, kb) in enumerate(UNITS)]

    def ends_tile(i):
        return 0 <= i < NS and units[i][4] == JB * (units[i][3] + 1) - 1

    def tile_of(i):
        return units[i][0] * NQT + units[i][3]

    flow = {i: [] for i in range(NS + 1)}
    for i, (s, g, u, qt, kb) in enumerate(units):
        if g == HYP_G and kb == 0:
            flow[i] += [("spread", qt, h) for h in range(G)]
        flow[i] += side[s, u]
        if ends_tile(i):
            flow[min(i + 2, NS)].append(("untranspose", tile_of(i)))
    order = [t for i in range(NS + 1) for t in flow[i]]
    banked = [t for t in order if t[0] in BANKED]
    NB = len(banked)
    bank_of = {t: n for n, t in enumerate(banked)}
    splits = [t for t in order if t[0] == "split"]
    hyp_units = [i for i, x in enumerate(units) if x[1] == HYP_G]
    diag_hyp = [i for i in hyp_units if units[i][4] >= JB * units[i][3]]
    NHP, NMASK = 2 * len(hyp_units), 2 * len(diag_hyp)
    last_rows = {g: max(n for t, n in bank_of.items() if t[0] == "rows" and t[1] == g) for g in (0, 1)}

    S_READY0, E_READY0, PV0, TWO = NP, 2, NU + 2, 2

    ctx = ExitStack()
    with ctx:
        def sb(name, shape, dt=F32):
            return ctx.enter_context(nc.sbuf_tensor("b_" + name, shape, dt))

        def ps(name, shape, dt=F32):
            return ctx.enter_context(nc.psum_tensor("b_" + name, shape, dt))

        def sem(name):
            return ctx.enter_context(nc.semaphore("b_" + name))

        KS = sb("KS", [P, NG, G, T], BF16)
        QS = sb("QS", [P, NG, G, T], BF16)
        E = sb("E", [P, 2, G, QT])
        A = sb("A", [P, 2, G, QT])
        M = sb("M", [P, G, QT])
        V = sb("V", [P, 2, NT, G * 32])
        OS = sb("OS", [P, 2, QT])
        YT = sb("YT", [P, 2, JB, G * HD])
        RZ = sb("RZ", [P, 2, JB * G])
        mxp = sb("mxp", [P, JB * G, NQT])
        mrow = sb("mrow", [P, JB * G])
        mres = sb("mres", [P, JB * G])
        mparts = sb("mparts", [P, 2, JB * G, 3], BF16)
        mhyp = sb("mhyp", [P, NT, G])
        hw = sb("hw", [P, 2, NT, G])

        score = [ps(f"score{i}", [P, 2, QT]) for i in range(2)]
        obank = [ps(f"out{i}", [P, QT]) for i in range(2)]
        sbank = [ps(f"side{i}", [P, QT]) for i in range(2)]

        stack_loaded = [sem(f"stack_loaded{s}") for s in range(NG)]
        v_loaded = [sem(f"v_loaded{i}") for i in range(2)]
        y_stored = [sem(f"y_stored{i}") for i in range(2)]
        s_ready, taken, e_ready, pv_done, os_ready, side_ready, side_free = map(
            sem, ["s_ready", "taken", "e_ready", "pv_done", "os_ready", "side_ready", "side_free"])
        storing = sem("storing")
        rz_ready, split_step, least_done, hyp_dve, hyp_act, mask_step = map(
            sem, ["rz_ready", "split_step", "least_done", "hyp_dve", "hyp_act", "mask_step"])
        sq_done, ln1_done, root_done, sum_done, ln2_done, ln3_done, rec_done, sub_done = map(
            sem, ["sq_done", "ln1_done", "root_done", "sum_done", "ln2_done", "ln3_done", "rec_done", "sub_done"])

        def first_query(i):
            return max(0, units[i][4] - JB * units[i][3]) * P

        def on_diagonal(i):
            return units[i][4] >= JB * units[i][3]

        STACK_DMAS = 2 * 12

        with nc.Block() as block:
            @block.sync
            def _(sp):
                def load_stack(b, first, s, g):
                    for qk, (dst, part) in enumerate([(QS, Q_PART), (KS, K_PART)]):
                        src = d["parts_h"][first:, :, :, :, :][bass.ds(b, 1), qk, G * g:G * g + G, :, :]
                        for slot in range(6):
                            r = PW * part[slot]
                            sp.dma_start(dst[HD * slot:HD * slot + HD, s, :, :],
                                         src[:, :, r:r + HD, :].rearrange("o h r t -> (o r) h t")
                                         ).then_inc(stack_loaded[s], 16)
                            sp.dma_start(dst[6 * HD + slot:6 * HD + slot + 1, s, :, :],
                                         src[:, :, r + HD:r + HD + 1, :].rearrange("o h r t -> (o r) h t")
                                         ).then_inc(stack_loaded[s], 16)

                def load_v(b, first, s, g):
                    sp.dma_start(V[:, s % 2, :, :], d["v_dram"][first:, :, :, :, :][bass.ds(b, 1), g, :, :, :].rearrange(
                        "o p n x -> (o p) n x")).then_inc(v_loaded[s % 2], 16)

                def sequence(b, more):
                    for s, g in enumerate(ORDER):
                        for qt in range(NQT):
                            tile = s * NQT + qt
                            n = bank_of["untranspose", tile]
                            sp.wait_ge(side_free, b * NB + n + 1 + TWO)
                            if qt == 0:
                                sp.sem_inc(storing, 1)
                            sp.dma_start(
                                d["y_dram"][bass.ds(b, 1), qt * QT:(qt + 1) * QT, 64 * g:64 * g + 64].rearrange(
                                    "o (j p) c -> p (o j) c", p=P), YT[:, tile % 2, :, :]
                            ).then_inc(y_stored[tile % 2], 16)
                        sp.wait_ge(pv_done, b * NS + (s + 1) * NU + PV0)
                        if s + 2 < NG:
                            load_v(b, 0, s + 2, ORDER[s + 2])
                        elif more:
                            load_v(b, 1, s + 2 - NG, ORDER[s + 2 - NG])
                        if more:
                            load_stack(b, 1, s, g)

                for i in range(2):
                    sp.sem_inc(y_stored[i], 16)
                for s, g in enumerate(ORDER):
                    load_stack(0, 0, s, g)
                    if s < 2:
                        load_v(0, 0, s, g)
                with sp.Fori(0, B - 1) as b:
                    sequence(b, True)
                sequence(B - 1, False)
                for i in range(2):
                    sp.wait_ge(y_stored[i], 16 + 16 * B * NTILE // 2)

            @block.tensor
            def _(pe):
                t = nc.tensor
                pe.sem_inc(s_ready, S_READY0)
                pe.sem_inc(pv_done, PV0)
                with pe.Fori(0, B) as b:
                    def scores(i, half):
                        s, g, u, qt, kb = units[i]
                        p = 2 * i + half
                        if u == 0 and half == 0:
                            pe.wait_ge(stack_loaded[s], (b + 1) * 16 * STACK_DMAS)
                            if g in last_rows:
                                pe.wait_ge(side_free, b * NB + last_rows[g] + 1 + TWO)
                        if p >= 2 and units[(p - 2) // 2][1] == HYP_G:
                            pe.wait_ge(taken, b * NHP + p - 2 - 2 * hyp_units[0] + 1)
                        else:
                            pe.wait_ge(e_ready, b * NP + p - 2 + 1 + E_READY0)
                        c0 = first_query(i)
                        masked = on_diagonal(i) and g != HYP_G
                        for x in range(2):
                            h = 2 * half + x
                            ins = t.matmul(score[half][:, x, c0:QT], KS[0:KROWS, s, h, kb * P:(kb + 1) * P],
                                           QS[0:KROWS, s, h, qt * QT + c0:(qt + 1) * QT], start=True,
                                           stop=not masked)
                            if masked:
                                ins = t.matmul(score[half][:, x, c0:c0 + P], k["neg_lowb"][:, :],
                                               k["identb"][:, :], start=False, stop=True)
                        ins.then_inc(s_ready, 1)

                    def values(i):
                        s, g, u, qt, kb = units[i]
                        tile = tile_of(i)
                        if u == 0:
                            pe.wait_ge(v_loaded[s % 2], b * 32 + 16 * (s // 2) + 16)
                        if kb == 0:
                            pe.wait_ge(os_ready, b * NTILE + tile - 2 + 1 + TWO)
                        pe.wait_ge(e_ready, b * NP + 2 * i + 2 + E_READY0)
                        c0 = first_query(i)
                        for h in range(G):
                            ins = t.matmul(obank[tile % 2][32 * h:32 * h + 32, c0:QT],
                                           V[:, s % 2, kb, 32 * h:32 * h + 32], E[:, i % 2, h, c0:QT],
                                           start=(kb == 0), stop=ends_tile(i))
                        ins.then_inc(pv_done, 1)

                    def side_task(task):
                        if task[0] == "split":
                            return
                        n = bank_of[task]
                        out = sbank[n % 2]
                        pe.wait_ge(side_free, b * NB + n - 2 + 1 + TWO)
                        if task[0] == "chunk":
                            _, g, qt, j, c, h = task
                            s = step_of[g]
                            if (qt, j, c, h) == (0, 0, 0, 0):
                                pe.wait_ge(stack_loaded[s], (b + 1) * 16 * STACK_DMAS)
                            diag = c == qt
                            wide = (j + 1) * P if diag else QT
                            q = qt * QT + j * P
                            ins = t.matmul(out[:, 0:wide], QS[0:KROWS, s, h, q:q + P],
                                           KS[0:KROWS, s, h, c * QT:c * QT + wide], start=True, stop=not diag)
                            if diag:
                                mask = k["pos_upb"] if g == HYP_G else k["neg_upb"]
                                ins = t.matmul(out[:, j * P:(j + 1) * P], mask[:, :], k["identb"][:, :],
                                               start=False, stop=True)
                        elif task[0] == "rows":
                            _, g, qt, hp = task
                            m = splits.index(("split", g, qt))
                            pe.wait_ge(split_step, (b * len(splits) + m + 1) * MSPLIT)
                            for x in range(2):
                                for j in range(JB):
                                    c = (x * JB + j) * P
                                    ins = t.transpose(out[:, :].bitcast(BF16)[96:99, c:c + P],
                                                      mparts[:, m % 2, j * G + 2 * hp + x, :], k["identb"][:, :])
                        elif task[0] == "spread":
                            _, qt, h = task
                            pe.wait_ge(hyp_act, (b + 1) * HYP_ACT)
                            for j in range(JB):
                                ins = t.matmul(out[:, j * P:(j + 1) * P],
                                               mhyp[:, qt * JB + j, h:h + 1].to_broadcast([P, P]), k["ident"][:, :],
                                               start=True, stop=True)
                        else:
                            tile = task[1]
                            pe.wait_ge(os_ready, b * NTILE + tile + 1 + TWO)
                            for j in range(JB):
                                ins = t.transpose(out[:, j * P:(j + 1) * P], OS[:, tile % 2, j * P:(j + 1) * P],
                                                  k["ident"][:, :])
                        ins.then_inc(side_ready, 1)

                    for half in range(2):
                        scores(0, half)
                    for i, (s, g, u, qt, kb) in enumerate(units):
                        if i + 1 < NS:
                            scores(i + 1, 0)
                            if g != HYP_G:
                                scores(i + 1, 1)
                        for task in flow[i]:
                            side_task(task)
                        if i + 1 < NS and g == HYP_G:
                            scores(i + 1, 1)
                        values(i)
                    for task in flow[NS]:
                        side_task(task)

            @block.scalar
            def _(act):
                a = nc.scalar
                act.sem_inc(e_ready, E_READY0)
                a.preload_act_table_set("natural_log_exp_and_others")
                with act.Fori(0, B) as b:
                    def largest_scores():
                        act.wait_ge(hyp_dve, b * HYP_DVE + 2)
                        a.activation(hw[:, 0, :, :], hw[:, 0, :, :], ACT.Ln, bias=k["m_one"][:, :]).then_inc(hyp_act, 1)
                        act.wait_ge(hyp_act, b * HYP_ACT + 1)
                        a.activation(hw[:, 0, :, :], hw[:, 0, :, :], ACT.Exp, scale=0.5).then_inc(hyp_act, 1)
                        act.wait_ge(hyp_dve, b * HYP_DVE + 3)
                        a.activation(hw[:, 1, :, :], hw[:, 1, :, :], ACT.Ln).then_inc(hyp_act, 1)
                        act.wait_ge(hyp_dve, b * HYP_DVE + 5)
                        a.activation(hw[:, 1, :, :], hw[:, 1, :, :], ACT.Ln).then_inc(hyp_act, 1)
                        act.wait_ge(hyp_act, b * HYP_ACT + 4)
                        a.activation(mhyp[:, :, :], hw[:, 1, :, :], ACT.Exp, scale=-1.0).then_inc(hyp_act, 1)

                    def exp_unit(i):
                        c0 = first_query(i)
                        act.wait_ge(pv_done, b * NS + i - 2 + 1 + PV0)
                        for half in range(2):
                            act.wait_ge(s_ready, b * NP + 2 * i + half + 1 + S_READY0)
                            a.activation(E[:, i % 2, 2 * half:2 * half + 2, c0:QT], score[half][:, :, c0:QT],
                                         ACT.Exp).then_inc(e_ready, 1)

                    def hyp_stage(i, buf, wait, done, func, **more):
                        n = b * NHP + 2 * hyp_units.index(i)
                        for half in range(2):
                            x = buf[:, i % 2, 2 * half:2 * half + 2, first_query(i):QT]
                            act.wait_ge(wait, n + half + 1)
                            a.activation(x, x, func, **more).then_inc(done, 1)

                    def root(i):
                        hyp_stage(i, E, sq_done, ln1_done, ACT.Ln, bias=k["m_one"][:, :])
                        hyp_stage(i, E, ln1_done, root_done, ACT.Exp, scale=0.5)

                    def inverse(i):
                        hyp_stage(i, A, sum_done, ln2_done, ACT.Ln)
                        n = b * NHP + 2 * hyp_units.index(i)
                        for half in range(2):
                            act.wait_ge(ln2_done, n + half + 1)
                            for h in range(2 * half, 2 * half + 2):
                                x = A[:, i % 2, h, first_query(i):QT]
                                ins = a.activation(x, x, ACT.Ln, bias=k["eps_dis"][:, :], scale=k["root"][:, h:h + 1])
                            ins.then_inc(ln3_done, 1)
                        hyp_stage(i, A, ln3_done, rec_done, ACT.Exp, scale=-1.0)

                    def exp_hyp(i):
                        hyp_stage(i, E, sub_done, e_ready, ACT.Exp)

                    for i, (s, g, u, qt, kb) in enumerate(units):
                        if g != HYP_G:
                            exp_unit(i)
                            continue
                        if u == 0:
                            largest_scores()
                        root(i)
                        if u:
                            exp_hyp(i - 1)
                        inverse(i)
                        if u == NU - 1:
                            exp_hyp(i)

            @block.gpsimd
            def _(pool):
                with pool.Fori(0, B) as b:
                    for n, i in enumerate(hyp_units):
                        c0 = first_query(i)
                        pool.wait_ge(pv_done, b * NS + i - 2 + 1 + PV0)
                        for half in range(2):
                            x = A[:, i % 2, 2 * half:2 * half + 2, c0:QT]
                            pool.wait_ge(taken, b * NHP + 2 * n + half + 1)
                            nc.gpsimd.tensor_tensor(E[:, i % 2, 2 * half:2 * half + 2, c0:QT], x, x,
                                                    ALU.mult).then_inc(sq_done, 1)

            @block.vector
            def _(dve):
                v = nc.vector
                dve.sem_inc(os_ready, TWO)
                dve.sem_inc(side_free, TWO)
                with dve.Fori(0, B) as b:
                    def least_a():
                        w0, w1 = hw[:, 0, :, :], hw[:, 1, :, :]
                        dve.wait_ge(least_done, (b + 1) * NQT)
                        v.tensor_scalar(w1, mhyp[:, :, :], ARG_MIN, None, ALU.max).then_inc(hyp_dve, 1)
                        dve.wait_ge(hyp_dve, b * HYP_DVE + 1)
                        v.tensor_tensor(w0, w1, w1, ALU.mult).then_inc(hyp_dve, 1)
                        dve.wait_ge(hyp_act, b * HYP_ACT + 2)
                        v.tensor_tensor(w1, w1, w0, ALU.add).then_inc(hyp_dve, 1)
                        dve.wait_ge(hyp_act, b * HYP_ACT + 3)
                        v.tensor_tensor(w1, w1, k["root"][:, :].unsqueeze(1).to_broadcast([P, NT, G]),
                                        ALU.mult).then_inc(hyp_dve, 1)
                        dve.wait_ge(hyp_dve, b * HYP_DVE + 4)
                        v.tensor_scalar(w1, w1, 1e-6, None, ALU.add).then_inc(hyp_dve, 1)

                    def take(i, half):
                        c0 = first_query(i)
                        n = hyp_units.index(i)
                        if n >= 2:
                            dve.wait_ge(sub_done, b * NHP + 2 * (n - 2) + half + 1)
                        dve.wait_ge(s_ready, b * NP + 2 * i + half + 1 + S_READY0)
                        v.tensor_scalar(A[:, i % 2, 2 * half:2 * half + 2, c0:QT], score[half][:, :, c0:QT],
                                        ARG_MIN, None, ALU.max).then_inc(taken, 1)

                    def add_root(i, half):
                        dve.wait_ge(root_done, b * NHP + 2 * hyp_units.index(i) + half + 1)
                        hh, c0 = slice(2 * half, 2 * half + 2), first_query(i)
                        v.tensor_tensor(A[:, i % 2, hh, c0:QT], A[:, i % 2, hh, c0:QT], E[:, i % 2, hh, c0:QT],
                                        ALU.add).then_inc(sum_done, 1)

                    def subtract(i, half):
                        hh, c0 = slice(2 * half, 2 * half + 2), first_query(i)
                        if units[i][4] == 0:
                            dve.wait_ge(side_free, b * NB + bank_of["spread", units[i][3], G - 1] + 1 + TWO)
                        dve.wait_ge(rec_done, b * NHP + 2 * hyp_units.index(i) + half + 1)
                        ins = v.tensor_tensor(E[:, i % 2, hh, c0:QT], A[:, i % 2, hh, c0:QT], M[:, hh, c0:QT],
                                              ALU.subtract)
                        if on_diagonal(i):
                            ins.then_inc(mask_step, 1)
                            dve.wait_ge(mask_step, b * NMASK + 2 * diag_hyp.index(i) + half + 1)
                            x = E[:, i % 2, hh, c0:c0 + P]
                            ins = v.tensor_tensor(x, x, k["neg_up"][:, :].unsqueeze(1).to_broadcast([P, 2, P]),
                                                  ALU.add)
                        ins.then_inc(sub_done, 1)

                    def split(g, qt, before):
                        m = splits.index(("split", g, qt))
                        n = (b * len(splits) + m) * MSPLIT
                        nh = MAX_HEADS[g]


                        cols = mxp[:, :, :].rearrange("p (j h) c -> p j h c", h=G)[:, :, 0:nh, 0:qt + 1]
                        row = mrow[:, :].rearrange("p (j h) -> p j h", h=G)[:, :, 0:nh]
                        res = mres[:, :].rearrange("p (j h) -> p j h", h=G)[:, :, 0:nh]
                        part = mparts[:, m % 2, :, :].rearrange("p (j h) a -> p j h a", h=G)[:, :, 0:nh, :]
                        dve.wait_ge(side_free, b * NB + before + 1 + TWO)
                        v.tensor_reduce(row, cols, AX_X, ALU.max, negate=True).then_inc(split_step, 1)
                        dve.wait_ge(split_step, n + 1)
                        v.tensor_copy(part[:, :, :, 0], row).then_inc(split_step, 1)
                        dve.wait_ge(split_step, n + 2)
                        v.tensor_tensor(res, row, part[:, :, :, 0], ALU.subtract).then_inc(split_step, 1)
                        dve.wait_ge(split_step, n + 3)
                        v.tensor_copy(part[:, :, :, 1], res).then_inc(split_step, 1)
                        dve.wait_ge(split_step, n + 4)
                        v.tensor_tensor(part[:, :, :, 2], res, part[:, :, :, 1], ALU.subtract).then_inc(split_step, 1)

                    def side_task(task, before):
                        if task[0] == "split":
                            split(task[1], task[2], before)
                            return
                        n = bank_of[task]
                        src = sbank[n % 2]
                        dve.wait_ge(side_ready, b * NB + n + 1)
                        if task[0] == "chunk":
                            _, g, qt, j, c, h = task
                            wide = (j + 1) * P if c == qt else QT
                            v.tensor_reduce(mxp[:, j * G + h, c:c + 1], src[:, 0:wide], AX_X,
                                            ALU.min if g == HYP_G else ALU.max).then_inc(side_free, 1)
                            if g == HYP_G and (j, c, h) == (JB - 1, qt, G - 1):
                                dve.wait_ge(side_free, b * NB + n + 1 + TWO)
                                v.tensor_reduce(mhyp[:, qt * JB:(qt + 1) * JB, :].rearrange("p j h -> p (j h)"),
                                                mxp[:, :, 0:qt + 1], AX_X, ALU.min).then_inc(least_done, 1)
                                dve.wait_ge(least_done, b * NQT + qt + 1)
                        elif task[0] == "rows":
                            _, g, qt, hp = task
                            v.tensor_copy(QS[96:99, step_of[g], 2 * hp:2 * hp + 2, qt * QT:(qt + 1) * QT],
                                          src[:, :].bitcast(BF16)[96:99, :].rearrange("p (h t) -> p h t", h=2)
                                          ).then_inc(side_free, 1)
                        elif task[0] == "spread":
                            _, qt, h = task
                            if qt:
                                last = hyp_units.index(step_of[HYP_G] * NU + UNITS.index((qt, 0)))
                                dve.wait_ge(sub_done, b * NHP + 2 * last)
                            v.tensor_copy(M[:, task[2], :], src[:, :]).then_inc(side_free, 1)
                        else:
                            tile = task[1]
                            o = src[:, :].rearrange("p (a w) -> p a w", w=32)
                            v.reciprocal(RZ[:, tile % 2, :], o[:, :, HD]).then_inc(rz_ready, 1)
                            dve.wait_ge(rz_ready, b * NTILE + tile + 1)
                            dve.wait_ge(y_stored[tile % 2], (b * (NTILE // 2) + tile // 2 + 1) * 16)
                            v.tensor_tensor(YT[:, tile % 2, :, :].rearrange("p j (h e) -> p (j h) e", e=HD),
                                            o[:, :, 0:HD], RZ[:, tile % 2, :].unsqueeze(2).to_broadcast(
                                                [P, JB * G, HD]), ALU.mult).then_inc(side_free, 1)

                    def evacuate(i):
                        tile = tile_of(i)
                        dve.wait_ge(pv_done, b * NS + i + 1 + PV0)
                        v.tensor_copy(OS[:, tile % 2, :], obank[tile % 2][:, :]).then_inc(os_ready, 1)

                    before = -1
                    for i, (s, g, u, qt, kb) in enumerate(units):
                        if g == HYP_G:
                            if u == 0:
                                least_a()
                                take(i, 0)
                                take(i, 1)
                            add_root(i, 0)
                            add_root(i, 1)
                        if ends_tile(i - 1):
                            evacuate(i - 1)
                        if g == HYP_G and u + 1 < NU:
                            take(i + 1, 0)
                        for task in flow[i]:
                            side_task(task, before)
                            before = bank_of.get(task, before)
                        if g == HYP_G:
                            if u + 1 < NU:
                                take(i + 1, 1)
                            subtract(i, 0)
                            subtract(i, 1)
                    evacuate(NS - 1)
                    for task in flow[NS]:
                        side_task(task, before)


def block_experts(nc, k, d):
    ctx = ExitStack()
    with ctx:
        def sb(name, shape, dt=F32):
            return ctx.enter_context(nc.sbuf_tensor("c_" + name, shape, dt))

        def ps(name):
            return ctx.enter_context(nc.psum_tensor("c_" + name, [P, 512], F32))

        def sem(name):
            return ctx.enter_context(nc.semaphore("c_" + name))

        CW = C + 1
        PAD = C + 8
        wproj = sb("wproj", [P, 2, C])
        pb, gamma, beta = sb("pb", [P, C]), sb("gamma", [P, C]), sb("beta", [P, C])
        mu = sb("mu", [P, 2, SLOTS])
        mu_sq = sb("mu_sq", [P, 2, SLOTS])
        mu_norm = sb("mu_norm", [P, SLOTS])
        scale = sb("scale", [P, 1])
        ones = sb("ones", [P, P])
        w1 = sb("w1", [P, 2, E, HID])
        b1T = sb("b1T", [HID, E])
        w2 = sb("w2", [HID, E, C])
        b2r = sb("b2r", [P, 2, C])
        Y = sb("Y", [P, NT, C])
        X = sb("X", [P, NT, C])
        X2 = sb("X2", [P, NT, C])
        L = sb("L", [P, NT, C])
        XN = sb("XN", [P, NT, PAD])
        EC = sb("EC", [P, NT, SLOTS])
        ECT = sb("ECT", [P, 2, T])
        D = sb("D", [P, NT, SLOTS])
        yT = sb("yT", [P, 2, 2, P])
        N_ = sb("normed", [P, 2, C])
        stats = sb("stats", [P, NT, 6])
        st = sb("st", [P, 6, NT])
        hn = sb("hn", [P, 4, NT])
        nmax = sb("nmax", [P, NT])
        cmax = sb("cmax", [P, SLOTS])
        cmaxT = sb("cmaxT", [P, 2])
        rz = sb("rz", [P, 2])
        rzo = sb("rzo", [P, NT])
        SI = sb("SI", [P, 2, C])
        SIT = sb("SIT", [P, 2, SLOTS])
        HT = sb("HT", [HID, SLOTS])
        HG = sb("HG", [HID, SLOTS])
        SOT = sb("SOT", [P, 2, SLOTS])
        SO = sb("SO", [P, 2, PAD])

        tp_bank = [ps(f"tp{u}") for u in range(2)]
        mm_bank = [ps(f"mm{u}") for u in range(2)]
        et_bank = [ps(f"et{u}") for u in range(2)]
        si_bank = [ps(f"si{u}") for u in range(2)]

        (weights, filled, prep, mu_psum, mu_root, x_loaded, y_loaded, out_stored) = map(
            sem, ["weights", "filled", "prep", "mu_psum", "mu_root", "x_loaded", "y_loaded", "out_stored"])
        (yt_psum, yt_ready, ao_psum, ao_ready, bs_done, var_ready, std_ready, rstd_ready) = map(
            sem, ["yt_psum", "yt_ready", "ao_psum", "ao_ready", "bs_done", "var_ready", "std_ready", "rstd_ready"])
        (n_ready, x2_ready, hn_step, hn_root, len_root, xn_a, xn_b, xn_ready) = map(
            sem, ["n_ready", "x2_ready", "hn_step", "hn_root", "len_root", "xn_a", "xn_b", "xn_ready"])
        (xnt_psum, xnt_ready, l_psum, l_ready, nmax_ready, ec_ready, ect_psum, ect_ready) = map(
            sem, ["xnt_psum", "xnt_ready", "l_psum", "l_ready", "nmax_ready", "ec_ready", "ect_psum", "ect_ready"])
        (cmax_ready, cmaxT_psum, cmaxT_ready, cmb_psum, d_sub, d_ready, si_psum, si_step) = map(
            sem, ["cmax_ready", "cmaxT_psum", "cmaxT_ready", "cmb_psum", "d_sub", "d_ready", "si_psum", "si_step"])
        (sit_psum, sit_ready, h_psum, h_ready, hg_ready, sot_psum, sot_ready, so_psum, so_ready) = map(
            sem, ["sit_psum", "sit_ready", "h_psum", "h_ready", "hg_ready", "sot_psum", "sot_ready", "so_psum",
                  "so_ready"])
        (fo_psum, fo_step, fo_ready, n2_ready, out_ready) = map(
            sem, ["fo_psum", "fo_step", "fo_ready", "n2_ready", "out_ready"])

        storing = sem("storing")
        NW = 10 + E
        HNS = 11
        DC = 4
        ND = NT // DC

        def col(buf, n):
            return buf[:, bass.ds(n, 1), 0:C].rearrange("p o c -> p (o c)")

        with nc.Block() as block:
            @block.sync
            def _(sp):
                def load_y(b, first):
                    sp.dma_start(Y[:, :, :], d["y_dram"][first:, :, :][bass.ds(b, 1), :, :].rearrange(
                        "o (n p) c -> p (o n) c", p=P)).then_inc(y_loaded, 16)

                def load_x(b, first):
                    sp.dma_start(X[:, :, :], d["x"][first:, :, :][bass.ds(b, 1), :, :].rearrange(
                        "o (n p) c -> p (o n) c", p=P)).then_inc(x_loaded, 16)

                load_y(0, 0)
                for dst, src in [(wproj[:, :, :], d["wproj"].rearrange("(k p) n -> p k n", p=P)),
                                 (pb[:, :], d["pb"].partition_broadcast(P)),
                                 (mu[:, :, :], d["mu"].rearrange("(k p) e s -> p k (e s)", p=P)),
                                 (gamma[:, :], d["gamma"].partition_broadcast(P)),
                                 (beta[:, :], d["beta"].partition_broadcast(P)),
                                 (scale[:, :], d["scale"].partition_broadcast(P)),
                                 (w1[:, 0, :, :], d["w1"][:, 0:P, :].rearrange("e p h -> p e h")),
                                 (w1[:, 1, :, :], d["w1"][:, P:C, :].rearrange("e p h -> p e h")),
                                 (b1T[:, :], d["b1T"]),
                                 (w2[:, :, :], d["w2"].rearrange("e h c -> h e c"))]:
                    sp.dma_start(dst, src).then_inc(weights, 16)
                for e in range(E):
                    sp.dma_start(b2r[e % 8 * S:(e % 8 + 1) * S, e // 8, :],
                                 d["b2"][e, :].partition_broadcast(S)).then_inc(weights, 16)
                load_x(0, 0)

                def store(b):
                    for m in range(ND):
                        sp.wait_ge(out_ready, b * NT + (m + 1) * DC + 2)
                        if m == 0:
                            sp.sem_inc(storing, 1)
                        sp.dma_start(d["out"][bass.ds(b, 1), m * DC * P:(m + 1) * DC * P, :].rearrange(
                            "o (n p) c -> p (o n) c", p=P), X2[:, m * DC:(m + 1) * DC, :]).then_inc(out_stored, 16)

                with sp.Fori(0, B - 1) as b:
                    sp.wait_ge(yt_psum, b * NT + NT)
                    load_y(b, 1)
                    sp.wait_ge(x2_ready, b * NT + NT + 2)
                    load_x(b, 1)
                    store(b)
                store(B - 1)
                sp.wait_ge(out_stored, 16 * ND * (B + 1))

            @block.gpsimd
            def _(pool):
                g = nc.gpsimd
                pool.sem_inc(out_stored, 16 * ND)
                g.memset(ones[:, :], 1.0).then_inc(filled, 1)
                g.memset(XN[:, :, C:CW], 1.0).then_inc(filled, 1)
                g.memset(SO[:, :, C:CW], 1.0).then_inc(filled, 1)
                pool.wait_ge(weights, 16 * NW)
                with pool.Fori(0, B) as b:
                    with pool.Fori(0, NT // 2) as m:
                        for u in range(2):
                            i = b * NT + m * 2 + u
                            n = m * 2 + u
                            pool.wait_ge(xn_b, i + 1)
                            g.tensor_tensor(col(XN, n), col(XN, n), beta[:, :], ALU.add).then_inc(xn_ready, 1)

            @block.vector
            def _(dve):
                v = nc.vector
                dve.sem_inc(ao_ready, 2)
                dve.sem_inc(x2_ready, 2)
                dve.sem_inc(l_ready, 2)
                dve.sem_inc(fo_ready, 2)
                dve.sem_inc(out_ready, 2)
                dve.sem_inc(so_ready, 1)
                dve.wait_ge(weights, 16 * NW)
                dve.wait_ge(filled, 3)
                v.tensor_tensor(mu_sq[:, :, :], mu[:, :, :], mu[:, :, :], ALU.mult).then_inc(prep, 1)
                dve.wait_ge(mu_root, 1)
                v.tensor_scalar(mu_norm[:, :], mu_norm[:, :], 1e-12, None, ALU.max).then_inc(prep, 1)
                dve.wait_ge(prep, 2)
                v.reciprocal(mu_norm[:, :], mu_norm[:, :]).then_inc(prep, 1)
                dve.wait_ge(prep, 3)
                v.tensor_tensor(mu[:, :, :], mu[:, :, :], mu_norm[:, :].unsqueeze(1).to_broadcast([P, 2, SLOTS]),
                                ALU.mult).then_inc(prep, 1)

                with dve.Fori(0, B) as b:
                    steps = [0]

                    def step(ins):
                        steps[0] += 1
                        ins.then_inc(hn_step, 1)
                        dve.wait_ge(hn_step, b * HNS + steps[0])

                    with dve.Fori(0, NT // 2) as m:
                        for u in range(2):
                            i, n = b * NT + m * 2 + u, m * 2 + u
                            dve.wait_ge(ao_psum, i + 1 + 2)
                            v.tensor_tensor(col(L, n), mm_bank[u][:, 0:C], pb[:, :], ALU.add).then_inc(ao_ready, 1)
                        for u in range(2):
                            i, n = b * NT + m * 2 + u, m * 2 + u
                            dve.wait_ge(ao_ready, i + 1 + 2)
                            v.bn_stats(stats[:, bass.ds(n, 1), :].rearrange(
                                "p o s -> p (o s)"), col(L, n)).then_inc(bs_done, 1)
                    dve.wait_ge(bs_done, b * 4 * NT + NT)
                    layer_norm_stats(nc, dve, stats, st, b * 3, var_ready, std_ready, rstd_ready)
                    with dve.Fori(0, NT // 2) as m:
                        dve.wait_ge(x_loaded, b * 16 + 16)
                        dve.wait_ge(out_stored, (b + 1) * 16 * ND)
                        for u in range(2):
                            i, n = b * NT + m * 2 + u, m * 2 + u
                            dve.wait_ge(n_ready, i + 1)
                            v.tensor_tensor(col(X2, n), col(X, n), N_[:, u, :], ALU.add).then_inc(x2_ready, 1)
                        for u in range(2):
                            i, n = b * NT + m * 2 + u, m * 2 + u
                            dve.wait_ge(x2_ready, i + 1 + 2)
                            v.bn_stats(stats[:, bass.ds(n, 1), :].rearrange("p o s -> p (o s)"),
                                       col(X2, n)).then_inc(bs_done, 1)
                    dve.wait_ge(bs_done, b * 4 * NT + 2 * NT)
                    layer_norm_stats(nc, dve, stats, st, b * 3 + 1, var_ready, std_ready, rstd_ready)
                    dve.wait_ge(rstd_ready, (b * 3 + 2) * 2)
                    step(v.tensor_tensor(hn[:, 0, :], st[:, 3, :], st[:, 5, :], ALU.mult))
                    step(v.tensor_tensor(hn[:, 0, :], hn[:, 0, :], st[:, 5, :], ALU.mult))
                    dve.wait_ge(hn_root, b + 1)
                    step(v.reciprocal(hn[:, 2, :], hn[:, 1, :]))
                    step(v.tensor_tensor(hn[:, 3, :], st[:, 0, :], hn[:, 2, :], ALU.mult))
                    steps[0] += 1
                    v.tensor_tensor(hn[:, 2, :], st[:, 5, :], hn[:, 2, :], ALU.mult).then_inc(hn_step, 1)
                    with dve.Fori(0, NT // 2) as m:
                        for u in range(2):
                            i, n = b * NT + m * 2 + u, m * 2 + u
                            dve.wait_ge(xn_a, i + 1)
                            v.tensor_tensor(col(XN, n), col(XN, n), gamma[:, :], ALU.mult).then_inc(xn_b, 1)
                        for u in range(2):
                            i, n = b * NT + m * 2 + u, m * 2 + u
                            dve.wait_ge(xn_ready, i + 1)
                            v.bn_stats(stats[:, bass.ds(n, 1), :].rearrange("p o s -> p (o s)"),
                                       col(XN, n)).then_inc(bs_done, 1)
                    dve.wait_ge(bs_done, b * 4 * NT + 3 * NT)
                    pick = stats[:, :, :].rearrange("p n s -> p s n")
                    step(v.tensor_tensor(st[:, 0, :], pick[:, 1, :], pick[:, 1, :], ALU.mult))
                    step(v.tensor_tensor(st[:, 1, :], pick[:, 4, :], pick[:, 4, :], ALU.mult))
                    step(v.tensor_tensor(st[:, 0, :], st[:, 0, :], st[:, 1, :], ALU.add))
                    step(v.tensor_tensor(st[:, 1, :], pick[:, 2, :], pick[:, 5, :], ALU.add))
                    step(v.scalar_tensor_tensor(out=hn[:, 0, :], in0=st[:, 0, :], scalar=C / 2.0, in1=st[:, 1, :],
                                                op0=ALU.mult, op1=ALU.add))
                    dve.wait_ge(len_root, b + 1)
                    step(v.tensor_scalar(hn[:, 1, :], hn[:, 1, :], 1e-12, None, ALU.max))
                    v.reciprocal(hn[:, 0, :], hn[:, 1, :]).then_inc(prep, 1)
                    dve.wait_ge(prep, 4 + b * 2 + 1)
                    v.tensor_scalar(hn[:, 0, :], hn[:, 0, :], scale[:, :], None, ALU.mult).then_inc(prep, 1)
                    with dve.Fori(0, NT // 2) as m:
                        dve.wait_ge(prep, 4 + b * 2 + 2)
                        assert steps[0] == HNS
                        for u in range(2):
                            i, n = b * NT + m * 2 + u, m * 2 + u
                            dve.wait_ge(l_psum, i + 1 + 2)
                            v.tensor_scalar(col(L, n), mm_bank[u][:, 0:C], hn[:, 0, bass.ds(n, 1)], None,
                                            ALU.mult).then_inc(l_ready, 1)
                        for u in range(2):
                            i, n = b * NT + m * 2 + u, m * 2 + u
                            dve.wait_ge(l_ready, i + 1 + 2)
                            v.tensor_reduce(nmax[:, bass.ds(n, 1)], col(L, n), AX_X, ALU.max,
                                            negate=True).then_inc(nmax_ready, 1)
                    v.tensor_reduce(cmax[:, :], L[:, :, :].rearrange("p n s -> p s n"), AX_X,
                                    ALU.max).then_inc(cmax_ready, 1)
                    dve.wait_ge(cmaxT_psum, b + 1)
                    v.tensor_reduce(cmaxT[:, :], si_bank[0][:, 0:2 * P].rearrange("p (c t) -> p c t", c=2), AX_X,
                                    ALU.max).then_inc(cmaxT_ready, 1)
                    dve.wait_ge(cmb_psum, b + 1)
                    for m in range(ND):
                        t_ = slice(m * DC, (m + 1) * DC)
                        v.tensor_tensor(D[:, t_, :], L[:, t_, :], si_bank[1][:, 0:SLOTS].unsqueeze(1).to_broadcast(
                            [P, DC, SLOTS]), ALU.subtract).then_inc(d_sub, 1)
                    dve.wait_ge(si_psum, b + 1)
                    for c in range(2):
                        v.reciprocal(rz[:, c:c + 1], si_bank[c][:, C:CW]).then_inc(si_step, 1)
                    for c in range(2):
                        dve.wait_ge(si_step, b * 4 + c + 1)
                        v.tensor_scalar(SI[:, c, :], si_bank[c][:, 0:C], rz[:, c:c + 1], None,
                                        ALU.mult).then_inc(si_step, 1)
                    dve.wait_ge(sit_psum, b + 1)
                    v.tensor_copy(SIT[:, :, :].rearrange("p k s -> p (k s)"), et_bank[0][:, :]).then_inc(sit_ready, 1)
                    dve.wait_ge(h_psum, b + 1)
                    v.tensor_tensor(HT[:, :].rearrange("h (e s) -> h e s", s=S),
                                    et_bank[1][0:HID, 0:SLOTS].rearrange("h (e s) -> h e s", s=S),
                                    b1T[:, :].unsqueeze(2).to_broadcast([HID, E, S]), ALU.add).then_inc(h_ready, 1)
                    dve.wait_ge(sot_psum, b + 1)
                    v.tensor_copy(SOT[:, :, :].rearrange("p k s -> p (k s)"), et_bank[0][:, :]).then_inc(sot_ready, 1)
                    dve.wait_ge(so_psum, b + 1)
                    v.tensor_tensor(SO[:, :, 0:C], et_bank[1][:, :].rearrange("p (c d) -> p c d", c=2), b2r[:, :, :],
                                    ALU.add).then_inc(so_ready, 1)
                    with dve.Fori(0, NT // 2) as m:
                        for u in range(2):
                            i, n = b * NT + m * 2 + u, m * 2 + u
                            dve.wait_ge(fo_psum, i + 1)
                            v.reciprocal(rzo[:, bass.ds(n, 1)], mm_bank[u][:, C:CW]).then_inc(fo_step, 1)
                        for u in range(2):
                            i, n = b * NT + m * 2 + u, m * 2 + u
                            dve.wait_ge(fo_step, i + 1)
                            v.tensor_scalar(col(L, n), mm_bank[u][:, 0:C], rzo[:, bass.ds(n, 1)], None,
                                            ALU.mult).then_inc(fo_ready, 1)
                        for u in range(2):
                            i, n = b * NT + m * 2 + u, m * 2 + u
                            dve.wait_ge(fo_ready, i + 1 + 2)
                            v.bn_stats(stats[:, bass.ds(n, 1), :].rearrange("p o s -> p (o s)"),
                                       col(L, n)).then_inc(bs_done, 1)
                    dve.wait_ge(bs_done, b * 4 * NT + 4 * NT)
                    layer_norm_stats(nc, dve, stats, st, b * 3 + 2, var_ready, std_ready, rstd_ready)
                    with dve.Fori(0, NT // 2) as m:
                        for u in range(2):
                            i, n = b * NT + m * 2 + u, m * 2 + u
                            dve.wait_ge(n2_ready, i + 1)
                            v.tensor_tensor(col(X2, n), col(X2, n), N_[:, u, :], ALU.add).then_inc(out_ready, 1)

            @block.scalar
            def _(act):
                a = nc.scalar
                act.sem_inc(yt_ready, 2)
                act.sem_inc(xnt_ready, 2)
                act.sem_inc(ect_ready, 2)
                act.wait_ge(mu_psum, 1)
                a.activation(mu_norm[:, :], si_bank[0][:, 0:SLOTS], ACT.Sqrt).then_inc(mu_root, 1)

                def root_of_variance(r):
                    act.wait_ge(var_ready, r * VAR + VAR)
                    a.activation(st[:, 4, :], st[:, 3, :], ACT.Sqrt, bias=k["eps_ln"][:, :],
                                 scale=1.0 / C).then_inc(std_ready, 1)
                    act.wait_ge(rstd_ready, r * 2 + 2)

                with act.Fori(0, B) as b:
                    with act.Fori(0, NT // 2) as m:
                        for u in range(2):
                            i = b * NT + m * 2 + u
                            act.wait_ge(yt_psum, i + 1)
                            act.wait_ge(ao_psum, i + 1)
                            a.copy(yT[:, u, :, :].rearrange("p k t -> p (k t)"),
                                   tp_bank[u][:, 0:C]).then_inc(yt_ready, 1)
                    root_of_variance(b * 3)
                    with act.Fori(0, NT // 2) as m:
                        for u in range(2):
                            i, n = b * NT + m * 2 + u, m * 2 + u
                            act.wait_ge(x2_ready, i + 1)
                            a.activation(N_[:, u, :], col(L, n), ACT.Identity, bias=st[:, 0, bass.ds(n, 1)],
                                         scale=st[:, 5, bass.ds(n, 1)]).then_inc(n_ready, 1)
                    root_of_variance(b * 3 + 1)
                    act.wait_ge(hn_step, b * HNS + 2)
                    a.activation(hn[:, 1, :], hn[:, 0, :], ACT.Sqrt, bias=k["eps_ln"][:, :],
                                 scale=1.0 / C).then_inc(hn_root, 1)
                    act.wait_ge(hn_step, b * HNS + 5)
                    with act.Fori(0, NT // 2) as m:
                        for u in range(2):
                            i, n = b * NT + m * 2 + u, m * 2 + u
                            a.activation(col(XN, n), col(X2, n), ACT.Identity, bias=hn[:, 3, bass.ds(n, 1)],
                                         scale=hn[:, 2, bass.ds(n, 1)]).then_inc(xn_a, 1)
                    act.wait_ge(hn_step, b * HNS + 10)
                    a.activation(hn[:, 1, :], hn[:, 0, :], ACT.Sqrt).then_inc(len_root, 1)
                    with act.Fori(0, NT // 2) as m:
                        for u in range(2):
                            i, n = b * NT + m * 2 + u, m * 2 + u
                            act.wait_ge(xnt_psum, i + 1)
                            act.wait_ge(l_psum, i + 1)
                            a.copy(yT[:, u, :, :].rearrange("p k t -> p (k t)"),
                                   tp_bank[u][:, 0:C]).then_inc(xnt_ready, 1)
                        for u in range(2):
                            i, n = b * NT + m * 2 + u, m * 2 + u
                            act.wait_ge(nmax_ready, i + 1)
                            a.activation(col(EC, n), col(L, n), ACT.Exp,
                                         bias=nmax[:, bass.ds(n, 1)]).then_inc(ec_ready, 1)
                        for u in range(2):
                            i, n = b * NT + m * 2 + u, m * 2 + u
                            act.wait_ge(ect_psum, i + 1)
                            a.copy(ECT[:, :, bass.ds(m * 2 * P + u * P, P)],
                                   et_bank[u][:, 0:C].rearrange("p (c t) -> p c t", c=2)).then_inc(ect_ready, 1)
                    for m in range(ND):
                        act.wait_ge(d_sub, b * ND + m + 1)
                        x = D[:, m * DC:(m + 1) * DC, :]
                        a.activation(x, x, ACT.Exp).then_inc(d_ready, 1)
                    act.wait_ge(h_ready, b + 1)
                    a.activation(HG[:, :], HT[:, :], ACT.Gelu).then_inc(hg_ready, 1)
                    root_of_variance(b * 3 + 2)
                    with act.Fori(0, NT // 2) as m:
                        for u in range(2):
                            i, n = b * NT + m * 2 + u, m * 2 + u
                            act.wait_ge(out_ready, i + 1)
                            a.activation(N_[:, u, :], col(L, n), ACT.Identity, bias=st[:, 0, bass.ds(n, 1)],
                                         scale=st[:, 5, bass.ds(n, 1)]).then_inc(n2_ready, 1)

            @block.tensor
            def _(pe):
                t = nc.tensor
                pe.sem_inc(ao_psum, 2)
                pe.sem_inc(l_psum, 2)
                pe.wait_ge(prep, 1)
                for c in range(2):
                    ins = t.matmul(si_bank[0][:, 0:SLOTS], ones[:, :], mu_sq[:, c, :], start=(c == 0), stop=(c == 1))
                ins.then_inc(mu_psum, 1)
                pe.wait_ge(mu_root, 1)
                with pe.Fori(0, B) as b:
                    def product(out, lhs, rhs):
                        for c in range(2):
                            ins = t.matmul(out, lhs(c), rhs(c), start=(c == 0), stop=(c == 1))
                        return ins

                    def turn(out, src):
                        for c in range(2):
                            ins = t.transpose(out[:, c * P:(c + 1) * P], src[:, c * P:(c + 1) * P], k["ident"][:, :])
                        return ins

                    pe.wait_ge(y_loaded, b * 16 + 16)
                    pe.wait_ge(xnt_ready, b * NT + 2)
                    pe.wait_ge(fo_ready, b * NT + 2)
                    for n in range(NT + 1):
                        if n < NT:
                            pe.wait_ge(yt_ready, b * NT + n + 1)
                            turn(tp_bank[n % 2], Y[:, n, :]).then_inc(yt_psum, 1)
                        if n:
                            u = (n - 1) % 2
                            pe.wait_ge(yt_ready, b * NT + n + 2)
                            pe.wait_ge(ao_ready, b * NT + n)
                            product(mm_bank[u][:, 0:C], lambda c: yT[:, u, c, :],
                                    lambda c: wproj[:, c, :]).then_inc(ao_psum, 1)
                    pe.wait_ge(ao_ready, b * NT + NT + 2)

                    def turn_xn(m):
                        for n in (2 * m, 2 * m + 1):
                            pe.wait_ge(xn_ready, b * NT + n + 1)
                            pe.wait_ge(xnt_ready, b * NT + n + 1)
                            turn(tp_bank[n % 2], XN[:, n, :]).then_inc(xnt_psum, 1)

                    turn_xn(0)
                    for m in range(NT // 2):
                        for n in (2 * m, 2 * m + 1):
                            pe.wait_ge(xnt_ready, b * NT + n + 3)
                            pe.wait_ge(l_ready, b * NT + n + 1)
                            product(mm_bank[n % 2][:, 0:C], lambda c: yT[:, n % 2, c, :],
                                    lambda c: mu[:, c, :]).then_inc(l_psum, 1)
                        if m + 1 < NT // 2:
                            turn_xn(m + 1)
                        for n in (2 * m, 2 * m + 1):
                            if n == 0:
                                pe.wait_ge(so_ready, b + 1)
                            pe.wait_ge(ec_ready, b * NT + n + 1)
                            pe.wait_ge(ect_ready, b * NT + n + 1)
                            turn(et_bank[n % 2], EC[:, n, :]).then_inc(ect_psum, 1)
                    pe.wait_ge(cmax_ready, b + 1)
                    turn(si_bank[0], cmax[:, :]).then_inc(cmaxT_psum, 1)
                    pe.wait_ge(cmaxT_ready, b + 1)
                    for c in range(2):
                        ins = t.matmul(si_bank[1][:, c * P:(c + 1) * P], cmaxT[:, c:c + 1].to_broadcast([P, P]),
                                       k["ident"][:, :], start=True, stop=True)
                    ins.then_inc(cmb_psum, 1)
                    for n in range(NT):
                        if n % DC == 0:
                            pe.wait_ge(d_ready, b * ND + n // DC + 1)
                        if n == 0:
                            pe.wait_ge(d_sub, b * ND + ND)
                        for c in range(2):
                            ins = t.matmul(si_bank[c][:, 0:CW], D[:, n, c * P:(c + 1) * P], XN[:, n, 0:CW],
                                           start=(n == 0), stop=(n == NT - 1))
                    ins.then_inc(si_psum, 1)
                    pe.wait_ge(ect_ready, b * NT + NT + 2)
                    pe.wait_ge(si_step, b * 4 + 4)
                    for kk in range(2):
                        for c in range(2):
                            ins = t.transpose(et_bank[0][:, (kk * 2 + c) * P:(kk * 2 + c + 1) * P],
                                              SI[:, c, kk * P:(kk + 1) * P], k["ident"][:, :])
                    ins.then_inc(sit_psum, 1)
                    pe.wait_ge(sit_ready, b + 1)
                    for e in range(E):
                        ins = product(et_bank[1][0:HID, e * S:(e + 1) * S], lambda c: w1[:, c, e, :],
                                      lambda c: SIT[:, c, e * S:(e + 1) * S])
                    ins.then_inc(h_psum, 1)
                    pe.wait_ge(hg_ready, b + 1)
                    for e in range(E):
                        for kk in range(2):
                            ins = t.matmul(et_bank[0][:, kk * SLOTS + e * S:kk * SLOTS + (e + 1) * S],
                                           w2[:, e, kk * P:(kk + 1) * P], HG[:, e * S:(e + 1) * S], start=True,
                                           stop=True)
                    ins.then_inc(sot_psum, 1)
                    pe.wait_ge(sot_ready, b + 1)
                    for c in range(2):
                        for kk in range(2):
                            ins = t.transpose(et_bank[1][:, (c * 2 + kk) * P:(c * 2 + kk + 1) * P],
                                              SOT[:, kk, c * P:(c + 1) * P], k["ident"][:, :])
                    ins.then_inc(so_psum, 1)
                    pe.wait_ge(so_ready, b + 2)
                    pe.wait_ge(l_ready, b * NT + NT + 2)
                    for n in range(NT):
                        pe.wait_ge(fo_ready, b * NT + n + 1)
                        product(mm_bank[n % 2][:, 0:CW], lambda c: ECT[:, c, n * P:(n + 1) * P],
                                lambda c: SO[:, c, 0:CW]).then_inc(fo_psum, 1)


HEADS = [*range(N_STD), *range(N_STD + N_HYP, H), *range(N_STD, N_STD + N_HYP)]


def build(nc, **d):
    with ExitStack() as ctx:
        d["parts"] = nc.dram_tensor("parts", (B, 2, H // 2, 2 * HW3, T), BF16, kind="Internal").ap()
        d["parts_h"] = d["parts"].rearrange("b q a (x r) t -> b q (a x) r t", x=2)
        d["v_dram"] = nc.dram_tensor("v_dram", (B, NG, P, NT, G * 32), F32, kind="Internal").ap()
        d["y_dram"] = nc.dram_tensor("y_dram", (B, T, C), F32, kind="Internal").ap()
        k = build_constants(nc, ctx, d)
        block_constants(nc, ctx, k, d)
        block_project(nc, k, d)
        block_attend(nc, k, d)
        block_experts(nc, k, d)


def kernel(**inputs):
    import numpy as np
    import concourse.bacc as bacc
    from concourse.bass_utils import run_bass_kernel_spmd

    x = np.ascontiguousarray(inputs["L0_attn_x"])
    frequency = 1.0 / 10000.0 ** (np.arange(0, HD, 2, dtype=np.float32) / np.float32(HD))
    angle = np.outer(np.arange(T, dtype=np.float32), frequency.astype(np.float32)).astype(np.float32)
    arrays = {
        "x": x,
        "wqkv": inputs["L0_attn_qkv_w"].reshape(3, H, HD, C)[:, HEADS].reshape(3 * C, C).T,
        "wproj": inputs["L0_attn_proj_w"].reshape(C, H, HD)[:, HEADS].reshape(C, C).T,
        "pb": inputs["L0_attn_proj_b"],
        "curv": inputs["L0_attn_curvature"].reshape(N_HYP),
        "cos": np.cos(angle),
        "sin": np.sin(angle),
        "gamma": inputs["L0_ffn_ln_gamma"],
        "beta": inputs["L0_ffn_ln_beta"],
        "mu": inputs["L0_ffn_mu"],
        "scale": inputs["L0_ffn_scale"],
        "w1": inputs["L0_ffn_w1"],
        "b1T": inputs["L0_ffn_b1"].T,
        "w2": inputs["L0_ffn_w2"],
        "b2": inputs["L0_ffn_b2"],
    }
    arrays = {name: np.ascontiguousarray(a) for name, a in arrays.items()}
    nc = bacc.Bacc("TRN2", target_bir_lowering=False, num_devices=1)
    args = {name: nc.dram_tensor(name, a.shape, mybir.dt.from_np(a.dtype), kind="ExternalInput").ap()
            for name, a in arrays.items()}
    args["out"] = nc.dram_tensor("out", (B, T, C), F32, kind="ExternalOutput").ap()
    build(nc, **args)
    r = run_bass_kernel_spmd(nc, [arrays], core_ids=[0])
    return r.results[0]["out"]
```

```python
from contextlib import ExitStack

import concourse.bass as bass
from concourse import mybir

F32 = mybir.dt.float32
BF16 = mybir.dt.bfloat16
ALU = mybir.AluOpType
ACT = mybir.ActivationFunctionType
AX_X = mybir.AxisListType.X

B, T, C = 4, 2048, 256
P = 128
NT = T // P
H, HD = 16, 16
G = 4
NG = H // G
N_STD, N_COS, N_HYP = 6, 6, 4
E, S, HID = 16, 16, 64
SLOTS = E * S
KROWS = 6 * HD + 6
PW = HD + 1
HW3 = 3 * PW
QT = 512
NQT = T // QT
JB = QT // P
BIG = 1e30
LN_EPS = 1e-5
ARG_MIN = 1.0 + 1.1920929e-07

COS_G, MIX_G, STD_G, HYP_G = 2, 1, 0, 3
MAX_HEADS = {STD_G: 4, MIX_G: 2, COS_G: 0, HYP_G: 4}
UNITS = [(qt, kb) for qt in range(NQT) for kb in range(JB * (qt + 1))]
NU = len(UNITS)
PLAIN = [(g, qt, kb) for g in (COS_G, MIX_G, STD_G) for qt, kb in UNITS]
LEAD = 14
TAIL = 9
ROOM = 1100
ACT_PASSES = {"exp": 1, "root": 2, "inverse": 3, "add": 0, "subtract": 0, "values": 0}
DVE_PASSES = {"exp": 0, "root": 0, "inverse": 0, "add": 1, "subtract": 1, "values": 0}


def plan():
    units, stages = [], {}

    def at(i, what, n):
        stages.setdefault(i, []).append((what, n))

    places = [LEAD + k * (len(PLAIN) - TAIL - LEAD) // NU for k in range(NU)]
    places += [places[-1] + 3, places[-1] + 6]
    since, k = None, -1
    for j, unit in enumerate(PLAIN):
        if j in places:
            k, since = k + 1, 0
            if k < NU:
                at(len(units), "add", k - 1)
                at(len(units), "exp", k - 2)
                units.append((HYP_G,) + UNITS[k])
                since = 1
        if since == 0:
            at(len(units), "add", k - 1)
            at(len(units), "exp", k - 2)
        if since == (1 if k < NU else 0):
            at(len(units), "inverse", k - 1)
            at(len(units), "values", k - 2)
        if since == (2 if k < NU else 1):
            at(len(units), "root", k)
            at(len(units), "subtract", k - 1)
        units.append(unit)
        since = None if since is None else since + 1
    stages = {i: [(what, n) for what, n in found if 0 <= n < NU] for i, found in stages.items()}

    def work(unit):
        return G * (QT - max(0, unit[2] - JB * unit[1]) * P) + 400

    room = []
    for i, unit in enumerate(units):
        act, dve = (0, work(unit)) if unit[0] == HYP_G else (work(unit), 0)
        for what, n in stages.get(i, []):
            act += ACT_PASSES[what] * work((HYP_G,) + UNITS[n])
            dve += DVE_PASSES[what] * work((HYP_G,) + UNITS[n])
        room.append(max(0, act - dve) / ROOM)
    return units, stages, room


def side_plan(units, stages, room):
    where = {stage: i for i, found in stages.items() for stage in found}
    flow = {i: [] for i in range(len(units) + 3)}
    chain = {}
    for qt in range(NQT):
        k = UNITS.index((qt, 0))
        i = where["subtract", k - 1] + 1 if k else where["subtract", 0] - 2
        for h in range(G):
            flow[i + h // 2].append(("spread", qt, h))
        chain[qt] = i - 5
    tasks = []
    for qt in range(NQT):
        for g in (HYP_G, STD_G, MIX_G):
            due = chain[qt] if g == HYP_G else units.index((g, qt, 0)) - 3
            some = [("chunk", g, qt, j, c, h) for j in range(JB) for c in range(qt + 1)
                    for h in range(MAX_HEADS[g])]
            if g != HYP_G:
                some += [("split", g, qt)] + [("rows", g, qt, hp) for hp in range(MAX_HEADS[g] // 2)]
            tasks.append((due, g, some))
    i, left = CHUNK_START, room[CHUNK_START]
    for due, _, some in sorted(tasks, key=lambda t: t[:2]):
        for task in some:
            while left <= 0:
                i += 1
                left += room[i]
            assert i < due, (task, i, due)
            flow[i].append(task)
            left -= 1
    ends = []
    for g in range(NG):
        for qt in range(NQT):
            k = UNITS.index((qt, JB * (qt + 1) - 1))
            i = where["values", k] if g == HYP_G else units.index((g,) + UNITS[k])
            ends.append((i + 1, g, qt))
    ends.sort()
    for tile, (i, g, qt) in enumerate(ends):
        assert tile < 2 or ends[tile - 2][0] + 1 < i
        flow[i + 1].append(("untranspose", tile))
    return flow, chain, ends


U = 4
FAC = 12
BANKED = ("chunk", "rows", "spread", "untranspose")
CHUNK_START = 4


def build_constants(nc, ctx, d):
    def sb(name, shape, dt=F32):
        return ctx.enter_context(nc.sbuf_tensor("k_" + name, shape, dt))

    k = {}
    k["ident"] = sb("ident", [P, P])
    k["identb"] = sb("identb", [P, P], BF16)
    k["zero"] = sb("zero", [P, P])
    k["neg_up"] = sb("neg_up", [P, P])
    k["neg_upb"] = sb("neg_upb", [P, P], BF16)
    k["neg_lowb"] = sb("neg_lowb", [P, P], BF16)
    k["pos_upb"] = sb("pos_upb", [P, P], BF16)
    k["eps_ln"] = sb("eps_ln", [P, 1])
    k["eps_dis"] = sb("eps_dis", [P, 1])
    k["m_one"] = sb("m_one", [P, 1])
    k["curv"] = sb("curv", [P, N_HYP])
    k["inv_c"] = sb("inv_c", [P, N_HYP])
    k["root"] = sb("root", [P, N_HYP])
    return k


def block_constants(nc, ctx, k, d):
    const_made = ctx.enter_context(nc.semaphore("const_made"))
    curv_loaded = ctx.enter_context(nc.semaphore("curv_loaded"))
    inv_made = ctx.enter_context(nc.semaphore("inv_made"))
    with nc.Block() as block:
        @block.sync
        def _(sp):
            sp.dma_start(k["curv"][:, :], d["curv"].partition_broadcast(P)).then_inc(curv_loaded, 16)

        @block.gpsimd
        def _(pool):
            g = nc.gpsimd
            n = [0]

            def made(ins):
                n[0] += 1
                ins.then_inc(const_made, 1)
                pool.wait_ge(const_made, n[0])

            g.memset(k["eps_ln"][:, :], LN_EPS)
            g.memset(k["eps_dis"][:, :], 1e-6)
            g.memset(k["m_one"][:, :], -1.0)
            made(g.memset(k["zero"][:, :], 0.0))
            made(g.affine_select(out=k["ident"][:, :], in_=k["zero"][:, :], pattern=[[-1, P]],
                                 compare_op=ALU.not_equal, fill=1.0, base=0, channel_multiplier=1))
            made(g.affine_select(out=k["neg_up"][:, :], in_=k["zero"][:, :], pattern=[[1, P]],
                                 compare_op=ALU.is_ge, fill=-BIG, base=0, channel_multiplier=-1))
            made(g.affine_select(out=k["neg_upb"][:, :], in_=k["zero"][:, :], pattern=[[1, P]],
                                 compare_op=ALU.is_ge, fill=-BIG, base=0, channel_multiplier=-1))
            made(g.affine_select(out=k["pos_upb"][:, :], in_=k["zero"][:, :], pattern=[[1, P]],
                                 compare_op=ALU.is_ge, fill=BIG, base=0, channel_multiplier=-1))
            made(g.affine_select(out=k["neg_lowb"][:, :], in_=k["zero"][:, :], pattern=[[-1, P]],
                                 compare_op=ALU.is_ge, fill=-BIG, base=0, channel_multiplier=1))
            made(g.tensor_copy(k["identb"][:, :], k["ident"][:, :]))

        @block.vector
        def _(dve):
            dve.wait_ge(curv_loaded, 16)
            nc.vector.reciprocal(k["inv_c"][:, :], k["curv"][:, :]).then_inc(inv_made, 1)

        @block.scalar
        def _(act):
            act.wait_ge(inv_made, 1)
            nc.scalar.activation(k["root"][:, :], k["inv_c"][:, :], ACT.Sqrt)


def block_project(nc, k, d):
    ctx = ExitStack()
    with ctx:
        def sb(name, shape, dt=F32):
            return ctx.enter_context(nc.sbuf_tensor("a_" + name, shape, dt))

        def ps(name, dt=F32):
            return ctx.enter_context(nc.psum_tensor("a_" + name, [P, 2048 // (4 if dt == F32 else 2)], dt))

        def sem(name):
            return ctx.enter_context(nc.semaphore("a_" + name))

        w = sb("w", [P, 2, 3 * C])
        cos = sb("cos", [P, NT, 8])
        sin = sb("sin", [P, NT, 8])
        X = sb("X", [P, NT, C])
        xn = sb("xn", [P, U, C])
        xT = sb("xT", [P, U, 2, P])
        T1 = sb("T1", [P, U, 64, 8])
        T2 = sb("T2", [P, U, 64, 8])
        QK = sb("QK", [P, NT, 2 * C])
        SQ = sb("SQ", [P, 2 * NT, 10 * HD])
        V = sb("V", [P, NG, NT, G, PW])
        F = sb("F", [P, NT, 2, H])
        N2 = sb("N2", [P, 2 * NT, 10])
        RN = sb("RN", [P, NT, 2, N_COS])
        HN = sb("HN", [P, NT, 2, N_HYP])
        HT = sb("HT", [P, NT, 2, N_HYP])
        AU = sb("AU", [P, NT, 2, N_HYP])
        AR = sb("AR", [P, NT, 2, N_HYP])
        AP3 = sb("AP3", [P, NT, 2 * N_HYP, 3], BF16)
        stats = sb("stats", [P, NT, 6])
        st = sb("st", [P, 6, NT])
        QKS = T1[:, :, :, :].rearrange("p u (h x) f -> p u h (x f)", x=2)
        R = T2[:, :, :, :].rearrange("p u (h x) f -> p u h (x f)", x=2)
        ST = sb("ST", [P, U, 2 * H, HW3], BF16)
        TS = sb("TS", [P, 2, H // 2, T], BF16)

        halves = [ps(f"half{u}") for u in range(4)]
        qk_bank = [ps(f"qk{u}") for u in range(U)]
        xt_bank = [halves[u // 2][:, u % 2 * C:(u % 2 + 1) * C] for u in range(U)]
        v_bank = [halves[2 + u // 2][:, u % 2 * C:(u % 2 + 1) * C] for u in range(U)]
        tq_bank = [halves[u][:, :].bitcast(BF16) for u in range(U)]
        tk_bank = [qk_bank[u][:, :].bitcast(BF16) for u in range(U)]

        w_loaded, x_loaded = sem("w_loaded"), sem("x_loaded")
        filled = sem("filled")
        x_free, bs_done, var_ready, std_ready, rstd_ready = map(
            sem, ["x_free", "bs_done", "var_ready", "std_ready", "rstd_ready"])
        xn_ready, xt_psum, xt_ready, qkv_done, rot_done, qk_ready, v_ready = map(
            sem, ["xn_ready", "xt_psum", "xt_ready", "qkv_done", "rot_done", "qk_ready", "v_ready"])
        roots_ready, fac_step = map(sem, ["roots_ready", "fac_step"])
        sc_done, hi_done, r_done, mid_done, lo_done, aug_done, tp_done, evq_done, evk_done = map(
            sem, ["sc_done", "hi_done", "r_done", "mid_done", "lo_done", "aug_done", "tp_done", "evq_done",
                  "evk_done"])
        v_stored, parts_stored = sem("v_stored"), sem("parts_stored")
        NW = 3

        with nc.Block() as block:
            @block.sync
            def _(sp):
                sp.dma_start(w[:, :, :], d["wqkv"].rearrange("(k p) n -> p k n", p=P)).then_inc(w_loaded, 16)
                sp.dma_start(cos[:, :, :], d["cos"].rearrange("(n p) f -> p n f", p=P)).then_inc(w_loaded, 16)
                sp.dma_start(sin[:, :, :], d["sin"].rearrange("(n p) f -> p n f", p=P)).then_inc(w_loaded, 16)
                def load_x(b, first):
                    sp.dma_start(X[:, :, :], d["x"][first:, :, :][bass.ds(b, 1), :, :].rearrange(
                        "o (n p) c -> p (o n) c", p=P)).then_inc(x_loaded, 16)

                def sequence(b, more):
                    sp.wait_ge(v_ready, b * NT + NT + U)
                    sp.dma_start(d["v_dram"][bass.ds(b, 1), :, :, :, :].rearrange("o g p n x -> p (o g) n x"),
                                 V[:, :, :, :, :].rearrange("p g n h x -> p g n (h x)")).then_inc(v_stored, 16)
                    if more:
                        sp.wait_ge(x_free, b * NT + NT + 1)
                        load_x(b, 1)
                    sp.wait_ge(evq_done, b * NT + NT + U)
                    sp.wait_ge(evk_done, b * NT + NT + U)
                    for qk in range(2):
                        sp.dma_start(d["parts"][bass.ds(b, 1), qk, :, :, :].rearrange("o a r t -> r (o a) t"),
                                     TS[0:2 * HW3, qk, :, :]).then_inc(parts_stored, 16)

                load_x(0, 0)
                with sp.Fori(0, B - 1) as b:
                    sequence(b, True)
                sequence(B - 1, False)
                sp.wait_ge(v_stored, 16 * B + 16)
                sp.wait_ge(parts_stored, 32 * B + 32)

            @block.gpsimd
            def _(pool):
                g = nc.gpsimd
                g.memset(V[:, :, :, :, HD:PW], 1.0).then_inc(filled, 1)
                g.memset(ST[:, :, :, :], 1.0).then_inc(filled, 1)
                pool.wait_ge(filled, 2)
                for u in range(U):
                    g.memset(ST[:, u, 0:H, 3 * HD:HW3], 0.0).then_inc(filled, 1)
                g.memset(F[:, :, :, :], 1.0).then_inc(filled, 1)
                pool.wait_ge(filled, 3 + U)
                g.memset(F[:, :, 0, 0:N_STD], HD ** -0.5).then_inc(filled, 1)
                pool.wait_ge(filled, 4 + U)
                for h in range(N_HYP):
                    g.tensor_scalar(F[:, :, 1, 12 + h], F[:, :, 1, 12 + h], k["curv"][:, h:h + 1], -1.0,
                                    ALU.mult, ALU.mult).then_inc(filled, 1)
                with pool.Fori(0, B) as b:
                    with pool.Fori(0, NT // U) as m:
                        for u in range(U):
                            i = b * NT + m * U + u
                            pool.wait_ge(rot_done, i + 1 + U)
                            n = m * U + u
                            qk = QK[:, bass.ds(n, 1), :].rearrange("p o (a s f) -> p (o a) s f", s=2, f=8)
                            t1 = T1[:, u, :, :].rearrange("p (a s) f -> p a s f", s=2)
                            t2 = T2[:, u, :, :].rearrange("p (a s) f -> p a s f", s=2)
                            g.tensor_tensor(qk[:, :, 0, :], t1[:, :, 0, :], t2[:, :, 1, :], ALU.add)
                            g.tensor_tensor(qk[:, :, 1, :], t1[:, :, 1, :], t2[:, :, 0, :],
                                            ALU.subtract).then_inc(qk_ready, 1)
                    with pool.Fori(0, NT // U) as m:
                        pool.wait_ge(fac_step, (b + 1) * FAC)
                        for u in range(U):
                            i = b * NT + m * U + u
                            n = m * U + u
                            pool.wait_ge(tp_done, i + 1)
                            for qk_ in range(2):
                                o = ST[:, u, :, 3 * HD:HW3].rearrange("p (q h) a -> p q h a", q=2)
                                ins = g.tensor_copy(o[:, qk_, 12:16, :],
                                                    AP3[:, bass.ds(n, 1), qk_ * 4:qk_ * 4 + 4, :].rearrange(
                                                        "p o h a -> p (o h) a"))
                            ins.then_inc(aug_done, 1)

            @block.vector
            def _(dve):
                v = nc.vector
                dve.sem_inc(rot_done, U)
                dve.sem_inc(evq_done, U)
                dve.wait_ge(w_loaded, 16 * NW)
                dve.wait_ge(filled, 8 + U)
                with dve.Fori(0, B) as b:
                    with dve.Fori(0, NT) as n:
                        dve.wait_ge(x_loaded, b * 16 + 16)
                        v.bn_stats(stats[:, bass.ds(n, 1), :].rearrange("p o s -> p (o s)"),
                                   X[:, bass.ds(n, 1), :].rearrange("p o c -> p (o c)")).then_inc(bs_done, 1)
                    dve.wait_ge(bs_done, b * NT + NT)
                    layer_norm_stats(nc, dve, stats, st, b, var_ready, std_ready, rstd_ready)
                    with dve.Fori(0, NT // U) as m:
                        for u in range(U):
                            i = b * NT + m * U + u
                            n = m * U + u
                            dve.wait_ge(qkv_done, i + 1 + U)
                            dve.wait_ge(qk_ready, i + 1)
                            src = qk_bank[u][:, :].rearrange("p (a f) -> p a f", f=8)
                            v.tensor_tensor(T1[:, u, :, :], src,
                                            cos[:, bass.ds(n, 1), :].to_broadcast([P, 64, 8]), ALU.mult)
                            v.tensor_tensor(T2[:, u, :, :], src,
                                            sin[:, bass.ds(n, 1), :].to_broadcast([P, 64, 8]),
                                            ALU.mult).then_inc(rot_done, 1)
                    dve.wait_ge(qk_ready, b * NT + NT + U)
                    steps = [0]

                    def step(ins):
                        steps[0] += 1
                        ins.then_inc(fac_step, 1)

                    def wait_steps():
                        dve.wait_ge(fac_step, b * FAC + steps[0])

                    norm_of = QK[:, :, :].rearrange("p n (q c) -> p (n q) c", q=2)[:, :, N_STD * HD:C]
                    step(v.tensor_tensor(SQ[:, :, :], norm_of, norm_of, ALU.mult))
                    wait_steps()
                    step(v.tensor_reduce(N2[:, :, :], SQ[:, :, :].rearrange("p m (h e) -> p m h e", e=HD),
                                         AX_X, ALU.add))
                    wait_steps()
                    n2 = N2[:, :, :].rearrange("p (n q) h -> p n q h", q=2)
                    step(v.tensor_tensor(HN[:, :, :, :].rearrange("p n q h -> p (n q) h"), N2[:, :, 6:10],
                                         k["inv_c"][:, :].unsqueeze(1).to_broadcast([P, 2 * NT, N_HYP]), ALU.add))
                    dve.wait_ge(roots_ready, b + 1)
                    step(v.tensor_scalar(RN[:, :, :, :], RN[:, :, :, :], 1e-12, None, ALU.max))
                    step(v.tensor_copy(AU[:, :, 0, :], HT[:, :, 0, :]))
                    step(v.tensor_tensor(AU[:, :, 1, :], HT[:, :, 1, :],
                                         k["curv"][:, :].unsqueeze(1).to_broadcast([P, NT, N_HYP]), ALU.mult))
                    wait_steps()
                    step(v.reciprocal(F[:, :, :, 6:12], RN[:, :, :, :]))
                    aug = AU[:, :, :, :].rearrange("p n q h -> p n (q h)")
                    rest = AR[:, :, :, :].rearrange("p n q h -> p n (q h)")
                    step(v.tensor_copy(AP3[:, :, :, 0], aug))
                    wait_steps()
                    step(v.tensor_scalar(F[:, :, 0, 6:12], F[:, :, 0, 6:12], HD ** 0.5, None, ALU.mult))
                    step(v.tensor_tensor(rest, aug, AP3[:, :, :, 0], ALU.subtract))
                    wait_steps()
                    step(v.tensor_copy(AP3[:, :, :, 1], rest))
                    wait_steps()
                    step(v.tensor_tensor(AP3[:, :, :, 2], rest, AP3[:, :, :, 1], ALU.subtract))
                    assert steps[0] == FAC
                    with dve.Fori(0, NT // U) as m:
                        wait_steps()
                        dve.wait_ge(parts_stored, b * 32 + 32)
                        stv = [ST[:, u, :, 0:3 * HD].rearrange("p h (a w) -> p h a w", w=HD) for u in range(U)]
                        for u in range(U):
                            i = b * NT + m * U + u
                            n = m * U + u
                            dve.wait_ge(lo_done, i + 1)
                            dve.wait_ge(hi_done, i + 1)
                            v.tensor_tensor(QKS[:, u, :, :],
                                            QK[:, bass.ds(n, 1), :].rearrange("p o (h e) -> p (o h) e", e=HD),
                                            F[:, bass.ds(n, 1), :, :].rearrange("p o q h -> p (o q h)").unsqueeze(
                                                2).to_broadcast([P, 2 * H, HD]), ALU.mult).then_inc(sc_done, 1)
                        for u in range(U):
                            i = b * NT + m * U + u
                            dve.wait_ge(hi_done, i + 1 + U)
                            dve.wait_ge(mid_done, i + 1)
                            v.tensor_tensor(R[:, u, :, :], QKS[:, u, :, :], stv[u][:, :, 0, 0:HD],
                                            ALU.subtract).then_inc(r_done, 1)
                        for u in range(U):
                            i = b * NT + m * U + u
                            dve.wait_ge(mid_done, i + 1 + U)
                            v.tensor_tensor(stv[u][:, :, 2, 0:HD], R[:, u, :, :], stv[u][:, :, 1, 0:HD],
                                            ALU.subtract).then_inc(lo_done, 1)
                        for u in range(U):
                            i = b * NT + m * U + u
                            dve.wait_ge(tp_done, i + 1 + U)
                            v.tensor_copy(TS[0:2 * HW3, 0, :, bass.ds(m * U * P + u * P, P)],
                                          tq_bank[u][0:2 * HW3, :].rearrange("p (a t) -> p a t", t=P)
                                          ).then_inc(evq_done, 1)

            @block.scalar
            def _(act):
                a = nc.scalar
                act.sem_inc(x_free, 1)
                act.sem_inc(xt_ready, U)
                act.sem_inc(v_ready, U)
                act.sem_inc(hi_done, U)
                act.sem_inc(mid_done, U)
                act.sem_inc(evk_done, U)
                act.sem_inc(v_stored, 16)
                act.sem_inc(parts_stored, 32)
                act.wait_ge(filled, 8 + U)
                with act.Fori(0, B) as b:
                    act.wait_ge(var_ready, b * VAR + VAR)
                    a.activation(st[:, 4, :], st[:, 3, :], ACT.Sqrt, bias=k["eps_ln"][:, :],
                                 scale=1.0 / C).then_inc(std_ready, 1)
                    act.wait_ge(rstd_ready, b * 2 + 2)
                    act.wait_ge(v_stored, b * 16 + 16)
                    with act.Fori(0, NT // U) as m:
                        for u in range(U):
                            i = b * NT + m * U + u
                            n = m * U + u
                            act.wait_ge(xt_psum, i + 1)
                            a.activation(xn[:, u, :], X[:, bass.ds(n, 1), :].rearrange("p o c -> p (o c)"),
                                         ACT.Identity, bias=st[:, 0, bass.ds(n, 1)],
                                         scale=st[:, 5, bass.ds(n, 1)]).then_inc(xn_ready, 1)
                        for u in range(U):
                            i = b * NT + m * U + u
                            act.wait_ge(xt_psum, i + 1 - u + (u | 1) + U)
                            act.wait_ge(qkv_done, i + 1)
                            a.copy(xT[:, u, :, :].rearrange("p k t -> p (k t)"),
                                   xt_bank[u]).then_inc(xt_ready, 1)
                        for u in range(U):
                            i = b * NT + m * U + u
                            n = m * U + u
                            act.wait_ge(qkv_done, i + 1 - u + (u | 1) + U)
                            a.copy(V[:, :, bass.ds(n, 1), :, 0:HD].rearrange("p g o h e -> p g (o h) e"),
                                   v_bank[u].rearrange("p (g h e) -> p g h e", g=NG, e=HD)).then_inc(v_ready, 1)
                    act.wait_ge(xn_ready, b * NT + NT)
                    act.sem_inc(x_free, NT)
                    act.wait_ge(fac_step, b * FAC + 3)
                    a.activation(RN[:, :, :, :], N2[:, :, 0:6].rearrange("p (n q) h -> p n q h", q=2), ACT.Sqrt)
                    a.activation(HT[:, :, :, :], HN[:, :, :, :], ACT.Sqrt).then_inc(roots_ready, 1)
                    act.wait_ge(parts_stored, b * 32 + 32)
                    stv = [ST[:, u, :, 0:3 * HD].rearrange("p h (a w) -> p h a w", w=HD) for u in range(U)]
                    with act.Fori(0, NT // U) as m:
                        for u in range(U):
                            i = b * NT + m * U + u
                            act.wait_ge(sc_done, i + 1)
                            act.wait_ge(tp_done, i + 1)
                            a.copy(stv[u][:, :, 0, 0:HD], QKS[:, u, :, :]).then_inc(hi_done, 1)
                        for u in range(U):
                            i = b * NT + m * U + u
                            act.wait_ge(r_done, i + 1)
                            a.copy(stv[u][:, :, 1, 0:HD], R[:, u, :, :]).then_inc(mid_done, 1)
                        for u in range(U):
                            i = b * NT + m * U + u
                            act.wait_ge(tp_done, i + 1 + U)
                            a.copy(TS[0:2 * HW3, 1, :, bass.ds(m * U * P + u * P, P)],
                                   tk_bank[u][0:2 * HW3, :].rearrange("p (a t) -> p a t", t=P)
                                   ).then_inc(evk_done, 1)

            @block.tensor
            def _(pe):
                t = nc.tensor
                pe.sem_inc(xt_psum, U)
                pe.sem_inc(qkv_done, U)
                pe.sem_inc(qk_ready, U)
                pe.sem_inc(lo_done, U)
                pe.sem_inc(tp_done, U)
                pe.wait_ge(w_loaded, 16 * NW)
                with pe.Fori(0, B) as b:
                    with pe.Fori(0, NT // U) as m:
                        pe.wait_ge(evq_done, b * NT + U)
                        pe.wait_ge(evk_done, b * NT + U)
                        for u in range(U):
                            i = b * NT + m * U + u
                            pe.wait_ge(xn_ready, i + 1)
                            pe.wait_ge(xt_ready, i + 1 - u + (u | 1))
                            for c in range(2):
                                ins = t.transpose(xt_bank[u][:, c * P:(c + 1) * P], xn[:, u, c * P:(c + 1) * P],
                                                  k["ident"][:, :])
                            ins.then_inc(xt_psum, 1)
                        for u in range(U):
                            i = b * NT + m * U + u
                            pe.wait_ge(xt_ready, i + 1 + U)
                            pe.wait_ge(rot_done, i + 1)
                            pe.wait_ge(v_ready, i + 1 - u + (u | 1))
                            for c in range(2):
                                t.matmul(qk_bank[u][:, :], xT[:, u, c, :], w[:, c, 0:2 * C], start=(c == 0),
                                         stop=(c == 1))
                            for c in range(2):
                                ins = t.matmul(v_bank[u], xT[:, u, c, :], w[:, c, 2 * C:3 * C],
                                               start=(c == 0), stop=(c == 1))
                            ins.then_inc(qkv_done, 1)
                    with pe.Fori(0, NT // U) as m:
                        pe.wait_ge(xt_ready, b * NT + NT + U)
                        pe.wait_ge(rot_done, b * NT + NT + U)
                        for u in range(U):
                            i = b * NT + m * U + u
                            pe.wait_ge(lo_done, i + 1 + U)
                            pe.wait_ge(hi_done, i + 1 + U)
                            pe.wait_ge(mid_done, i + 1 + U)
                            pe.wait_ge(aug_done, i + 1)
                            pe.wait_ge(evq_done, i + 1)
                            pe.wait_ge(evk_done, i + 1)
                            st_ = ST[:, u, :, :].rearrange("p (a x) w -> p a (x w)", x=2)
                            for qk in range(2):
                                bank = (tq_bank, tk_bank)[qk][u]
                                for a in range(H // 2):
                                    ins = t.transpose(bank[0:2 * HW3, a * P:(a + 1) * P], st_[:, 8 * qk + a, :],
                                                      k["identb"][:, :])
                            ins.then_inc(tp_done, 1)


VAR = 5


def layer_norm_stats(nc, dve, stats, st, b, var_ready, std_ready, rstd_ready):
    v = nc.vector
    pick = stats[:, :, :].rearrange("p n s -> p s n")
    v.tensor_tensor(st[:, 0, :], pick[:, 1, :], pick[:, 4, :], ALU.add).then_inc(var_ready, 1)
    v.tensor_tensor(st[:, 1, :], pick[:, 1, :], pick[:, 4, :], ALU.subtract).then_inc(var_ready, 1)
    v.tensor_tensor(st[:, 2, :], pick[:, 2, :], pick[:, 5, :], ALU.add).then_inc(var_ready, 1)
    dve.wait_ge(var_ready, b * VAR + 3)
    v.tensor_tensor(st[:, 4, :], st[:, 1, :], st[:, 1, :], ALU.mult).then_inc(var_ready, 1)
    dve.wait_ge(var_ready, b * VAR + 4)
    v.scalar_tensor_tensor(out=st[:, 3, :], in0=st[:, 4, :], scalar=C / 4.0, in1=st[:, 2, :], op0=ALU.mult,
                           op1=ALU.add).then_inc(var_ready, 1)
    dve.wait_ge(std_ready, b + 1)
    v.reciprocal(st[:, 5, :], st[:, 4, :]).then_inc(rstd_ready, 1)
    dve.wait_ge(rstd_ready, b * 2 + 1)
    v.scalar_tensor_tensor(out=st[:, 0, :], in0=st[:, 0, :], scalar=-0.5, in1=st[:, 5, :], op0=ALU.mult,
                           op1=ALU.mult).then_inc(rstd_ready, 1)


NS = NG * NU
NTILE = NG * NQT
NPP = 2 * len(PLAIN)
NHP = 2 * NU
MSPLIT = 5
HYP_DVE, HYP_ACT = 5, 5


def block_attend(nc, k, d):
    units, stages, room = plan()
    flow, chain, ends = side_plan(units, stages, room)
    order = [t for i in range(NS + 3) for t in flow[i]]
    banked = [t for t in order if t[0] in BANKED]
    NB = len(banked)
    bank_of = {t: n for n, t in enumerate(banked)}
    splits = [t for t in order if t[0] == "split"]
    tile_of = {(g, qt): n for n, (_, g, qt) in enumerate(ends)}
    rank = {u: n for g in range(NG) for n, u in enumerate(
        [u for u in units if (u[0] == HYP_G) == (g == HYP_G)])}
    hyp_units = [i for i, u in enumerate(units) if u[0] == HYP_G]
    diag_hyp = [n for n, (qt, kb) in enumerate(UNITS) if kb >= JB * qt]
    NMASK = 2 * len(diag_hyp)

    S0, E0, PV0, TWO = 2 * NS, 2, len(PLAIN) + 2, 2

    ctx = ExitStack()
    with ctx:
        def sb(name, shape, dt=F32):
            return ctx.enter_context(nc.sbuf_tensor("b_" + name, shape, dt))

        def ps(name, shape, dt=F32):
            return ctx.enter_context(nc.psum_tensor("b_" + name, shape, dt))

        def sem(name):
            return ctx.enter_context(nc.semaphore("b_" + name))

        KS = sb("KS", [P, NG, G, T], BF16)
        QS = sb("QS", [P, NG, G, T], BF16)
        E = sb("E", [P, 2, G, QT])
        EH = sb("EH", [P, 2, G, QT])
        A = sb("A", [P, 2, G, QT])
        M = sb("M", [P, G, QT])
        V = sb("V", [P, 3, NT, G * PW])
        OS = sb("OS", [P, 2, QT])
        YT = sb("YT", [P, 2, JB, G * HD])
        RZ = sb("RZ", [P, 2, JB * G])
        mxp = sb("mxp", [P, JB * G, NQT])
        mrow = sb("mrow", [P, JB * G])
        mres = sb("mres", [P, JB * G])
        mparts = sb("mparts", [P, 2, JB * G, 3], BF16)
        mhyp = sb("mhyp", [P, NT, G])
        hw = sb("hw", [P, 2, NT, G])

        score = [ps(f"score{i}", [P, 2, QT]) for i in range(2)]
        obank = [ps(f"out{i}", [P, QT]) for i in range(2)]
        sbank = [ps(f"side{i}", [P, QT]) for i in range(2)]

        stack_loaded = [sem(f"stack_loaded{s}") for s in range(NG)]
        v_loaded = [sem(f"v_loaded{i}") for i in range(3)]
        V_OF = {COS_G: 0, MIX_G: 1, HYP_G: 2, STD_G: 0}
        y_stored = [sem(f"y_stored{i}") for i in range(2)]
        s_ready, taken, e_ready, x_ready, pv_done, pvh_done, os_ready, side_ready, side_free, banks_filled = map(
            sem, ["s_ready", "taken", "e_ready", "x_ready", "pv_done", "pvh_done", "os_ready", "side_ready",
                  "side_free", "banks_filled"])
        storing = sem("storing")
        rz_ready, split_step, least_done, hyp_dve, hyp_act, mask_step = map(
            sem, ["rz_ready", "split_step", "least_done", "hyp_dve", "hyp_act", "mask_step"])
        sq_done, ln1_done, root_done, sum_done, ln2_done, ln3_done, rec_done, sub_done = map(
            sem, ["sq_done", "ln1_done", "root_done", "sum_done", "ln2_done", "ln3_done", "rec_done", "sub_done"])

        def first_query(unit):
            return max(0, unit[2] - JB * unit[1]) * P

        def on_diagonal(unit):
            return unit[2] >= JB * unit[1]

        def stage(i, what):
            return [n for w, n in stages.get(i, []) if w == what]

        STACK_DMAS = 3 * 2 + 6 + 3

        with nc.Block() as block:
            @block.sync
            def _(sp):
                def load_stack(b, first, g):
                    q, kk = (d["parts_h"][first:, :, :, :, :][bass.ds(b, 1), qk, G * g:G * g + G, :, :]
                             for qk in range(2))
                    row = 0
                    for n in (3, 2, 1):
                        for to, r, rows in [(HD * row, 0, HD * n), (6 * HD + row, 3 * HD, n)]:
                            sp.dma_start(KS[to:to + rows, g, :, :],
                                         kk[:, :, r:r + rows, :].rearrange("o h r t -> (o r) h t")
                                         ).then_inc(stack_loaded[g], 16)
                        r = 3 - n
                        for slot in range(row, row + n):
                            sp.dma_start(QS[HD * slot:HD * slot + HD, g, :, :],
                                         q[:, :, HD * r:HD * r + HD, :].rearrange("o h r t -> (o r) h t")
                                         ).then_inc(stack_loaded[g], 16)
                        sp.dma_start(QS[6 * HD + row:6 * HD + row + n, g, :, :],
                                     q[:, :, 3 * HD + r, :].rearrange("o h t -> (o h) t").partition_broadcast(n)
                                     ).then_inc(stack_loaded[g], 16)
                        row += n

                def load_v(b, first, g):
                    sp.dma_start(V[:, V_OF[g], :, :], d["v_dram"][first:, :, :, :, :][bass.ds(b, 1), g, :, :, :].rearrange(
                        "o p n x -> (o p) n x")).then_inc(v_loaded[V_OF[g]], 16)

                def sequence(b, more):
                    for tile, (_, g, qt) in enumerate(ends):
                        if qt == NQT - 1 and (more or g == COS_G):
                            if g == HYP_G:
                                sp.wait_ge(pvh_done, (b + 1) * NU + TWO)
                            else:
                                sp.wait_ge(pv_done, b * len(PLAIN) + rank[g, *UNITS[-1]] + 1 + PV0)
                            if g == COS_G:
                                load_v(b, 0, STD_G)
                            elif more:
                                load_v(b, 1, COS_G if g == STD_G else g)
                            if more:
                                load_stack(b, 1, g)
                        n = bank_of["untranspose", tile]
                        sp.wait_ge(side_free, b * NB + n + 1 + TWO)
                        sp.sem_inc(storing, 1)
                        sp.dma_start(
                            d["y_dram"][bass.ds(b, 1), qt * QT:(qt + 1) * QT, 64 * g:64 * g + 64].rearrange(
                                "o (j p) c -> p (o j) c", p=P), YT[:, tile % 2, :, :]
                        ).then_inc(y_stored[tile % 2], 16)

                for i in range(2):
                    sp.sem_inc(y_stored[i], 16)
                for g in (COS_G, HYP_G, MIX_G, STD_G):
                    load_stack(0, 0, g)
                    if g != STD_G:
                        load_v(0, 0, g)
                with sp.Fori(0, B - 1) as b:
                    sequence(b, True)
                sequence(B - 1, False)
                for i in range(2):
                    sp.wait_ge(y_stored[i], 16 + 16 * B * NTILE // 2)

            @block.tensor
            def _(pe):
                t = nc.tensor
                pe.sem_inc(s_ready, S0)
                pe.sem_inc(pv_done, PV0)
                pe.sem_inc(pvh_done, TWO)
                pe.wait_ge(banks_filled, 2)
                with pe.Fori(0, B) as b:
                    def scores(i, half):
                        g, qt, kb = unit = units[i]
                        if (qt, kb, half) == (0, 0, 0):
                            pe.wait_ge(stack_loaded[g], (b + 1) * 16 * STACK_DMAS)
                        if kb == 0 and half == 0 and g in (STD_G, MIX_G):
                            n = bank_of["rows", g, qt, MAX_HEADS[g] // 2 - 1]
                            pe.wait_ge(side_free, b * NB + n + 1 + TWO)
                        if i and units[i - 1][0] == HYP_G:
                            pe.wait_ge(taken, b * NHP + 2 * rank[units[i - 1]] + half + 1)
                        else:
                            before = 2 * rank[units[i - 1]] - (0 if i else NPP)
                            pe.wait_ge(e_ready, b * NPP + before + half + 1 + E0)
                        c0 = first_query(unit)
                        masked = on_diagonal(unit) and g != HYP_G
                        for x in range(2):
                            h = 2 * half + x
                            ins = t.matmul(score[half][:, x, c0:QT], KS[0:KROWS, g, h, kb * P:(kb + 1) * P],
                                           QS[0:KROWS, g, h, qt * QT + c0:(qt + 1) * QT], start=True,
                                           stop=not masked)
                            if masked:
                                ins = t.matmul(score[half][:, x, c0:c0 + P], k["neg_lowb"][:, :],
                                               k["identb"][:, :], start=False, stop=True)
                        ins.then_inc(s_ready, 1)

                    def values(unit):
                        g, qt, kb = unit
                        n, hyp, tile = rank[unit], g == HYP_G, tile_of[g, qt]
                        if (qt, kb) == (0, 0):
                            if V_OF[g] == 0:
                                pe.wait_ge(v_loaded[0], b * 32 + (16 if g == COS_G else 32))
                            else:
                                pe.wait_ge(v_loaded[V_OF[g]], b * 16 + 16)
                        if kb == 0:
                            same = [m for m, x in enumerate(ends) if (x[1] == HYP_G) == hyp]
                            m = same.index(tile)
                            before = same[m - 1] if m else same[-1] - NTILE
                            pe.wait_ge(os_ready, b * NTILE + before + 1 + TWO)
                        if hyp:
                            pe.wait_ge(x_ready, b * NHP + 2 * n + 2)
                        else:
                            pe.wait_ge(e_ready, b * NPP + 2 * n + 2 + E0)
                        c0 = first_query(unit)
                        for h in range(G):
                            ins = t.matmul(obank[hyp][32 * h:32 * h + PW, c0:QT],
                                           V[:, V_OF[g], kb, PW * h:PW * h + PW], (EH if hyp else E)[:, n % 2, h, c0:QT],
                                           start=(kb == 0), stop=(kb == JB * (qt + 1) - 1))
                        ins.then_inc(pvh_done if hyp else pv_done, 1)

                    def side_task(task):
                        if task[0] == "split":
                            return
                        n = bank_of[task]
                        out = sbank[n % 2]
                        pe.wait_ge(side_free, b * NB + n - 2 + 1 + TWO)
                        if task[0] == "chunk":
                            _, g, qt, j, c, h = task
                            if (qt, j, c, h) == (0, 0, 0, 0):
                                pe.wait_ge(stack_loaded[g], (b + 1) * 16 * STACK_DMAS)
                            diag = c == qt
                            wide = (j + 1) * P if diag else QT
                            q = qt * QT + j * P
                            ins = t.matmul(out[:, 0:wide], QS[0:KROWS, g, h, q:q + P],
                                           KS[0:KROWS, g, h, c * QT:c * QT + wide], start=True, stop=not diag)
                            if diag:
                                mask = k["pos_upb"] if g == HYP_G else k["neg_upb"]
                                ins = t.matmul(out[:, j * P:(j + 1) * P], mask[:, :], k["identb"][:, :],
                                               start=False, stop=True)
                        elif task[0] == "rows":
                            _, g, qt, hp = task
                            m = splits.index(("split", g, qt))
                            pe.wait_ge(split_step, (b * len(splits) + m + 1) * MSPLIT)
                            for x in range(2):
                                for j in range(JB):
                                    c = (x * JB + j) * P
                                    ins = t.transpose(out[:, :].bitcast(BF16)[96:99, c:c + P],
                                                      mparts[:, m % 2, j * G + 2 * hp + x, :], k["identb"][:, :])
                        elif task[0] == "spread":
                            _, qt, h = task
                            pe.wait_ge(hyp_act, (b * NQT + qt + 1) * HYP_ACT)
                            for j in range(JB):
                                ins = t.matmul(out[:, j * P:(j + 1) * P],
                                               mhyp[:, qt * JB + j, h:h + 1].to_broadcast([P, P]), k["ident"][:, :],
                                               start=True, stop=True)
                        else:
                            tile = task[1]
                            pe.wait_ge(os_ready, b * NTILE + tile + 1 + TWO)
                            for j in range(JB):
                                ins = t.transpose(out[:, j * P:(j + 1) * P], OS[:, tile % 2, j * P:(j + 1) * P],
                                                  k["ident"][:, :])
                        ins.then_inc(side_ready, 1)

                    scores(0, 0)
                    scores(0, 1)
                    for i, unit in enumerate(units):
                        some = (len(flow[i]) + 1) // 2
                        if i + 1 < NS:
                            scores(i + 1, 0)
                        for task in flow[i][:some]:
                            side_task(task)
                        for n in stage(i, "values"):
                            values((HYP_G,) + UNITS[n])
                        if i + 1 < NS:
                            scores(i + 1, 1)
                        more = (some + len(flow[i]) + 1) // 2
                        for task in flow[i][some:more]:
                            side_task(task)
                        if unit[0] != HYP_G:
                            values(unit)
                        for task in flow[i][more:]:
                            side_task(task)
                    for i in range(NS, NS + 3):
                        for task in flow[i]:
                            side_task(task)

            @block.scalar
            def _(act):
                a = nc.scalar
                act.sem_inc(e_ready, E0)
                a.preload_act_table_set("natural_log_exp_and_others")
                with act.Fori(0, B) as b:
                    def largest_scores(qt, part):
                        n, m = (b * NQT + qt) * HYP_DVE, (b * NQT + qt) * HYP_ACT
                        j = slice(qt * JB, (qt + 1) * JB)
                        w0, w1 = hw[:, 0, j, :], hw[:, 1, j, :]
                        if part == 1:
                            act.wait_ge(hyp_dve, n + 2)
                            a.activation(w0, w0, ACT.Ln, bias=k["m_one"][:, :]).then_inc(hyp_act, 1)
                            act.wait_ge(hyp_act, m + 1)
                            a.activation(w0, w0, ACT.Exp, scale=0.5).then_inc(hyp_act, 1)
                        elif part == 2:
                            act.wait_ge(hyp_dve, n + 3)
                            a.activation(w1, w1, ACT.Ln).then_inc(hyp_act, 1)
                        elif part == 3:
                            act.wait_ge(hyp_dve, n + 5)
                            a.activation(w1, w1, ACT.Ln).then_inc(hyp_act, 1)
                            act.wait_ge(hyp_act, m + 4)
                            a.activation(mhyp[:, j, :], w1, ACT.Exp, scale=-1.0).then_inc(hyp_act, 1)

                    def exp_plain(i):
                        n, c0 = rank[units[i]], first_query(units[i])
                        act.wait_ge(pv_done, b * len(PLAIN) + n - 2 + 1 + PV0)
                        for half in range(2):
                            act.wait_ge(s_ready, b * 2 * NS + 2 * i + half + 1 + S0)
                            a.activation(E[:, n % 2, 2 * half:2 * half + 2, c0:QT], score[half][:, :, c0:QT],
                                         ACT.Exp).then_inc(e_ready, 1)

                    def in_place(n, buf, wait, done, func, **more):
                        for half in range(2):
                            x = buf[:, n % 2, 2 * half:2 * half + 2, first_query((HYP_G,) + UNITS[n]):QT]
                            act.wait_ge(wait, b * NHP + 2 * n + half + 1)
                            a.activation(x, x, func, **more).then_inc(done, 1)

                    def root(n):
                        in_place(n, EH, sq_done, ln1_done, ACT.Ln, bias=k["m_one"][:, :])
                        in_place(n, EH, ln1_done, root_done, ACT.Exp, scale=0.5)

                    def inverse(n):
                        in_place(n, A, sum_done, ln2_done, ACT.Ln)
                        for half in range(2):
                            act.wait_ge(ln2_done, b * NHP + 2 * n + half + 1)
                            for h in range(2 * half, 2 * half + 2):
                                x = A[:, n % 2, h, first_query((HYP_G,) + UNITS[n]):QT]
                                ins = a.activation(x, x, ACT.Ln, bias=k["eps_dis"][:, :], scale=k["root"][:, h:h + 1])
                            ins.then_inc(ln3_done, 1)
                        in_place(n, A, ln3_done, rec_done, ACT.Exp, scale=-1.0)

                    for i, unit in enumerate(units):
                        for n in stage(i, "exp"):
                            in_place(n, EH, sub_done, x_ready, ACT.Exp)
                        if unit[0] != HYP_G:
                            exp_plain(i)
                        for n in stage(i, "inverse"):
                            inverse(n)
                        for n in stage(i, "root"):
                            root(n)
                        for qt in range(NQT):
                            largest_scores(qt, i - chain[qt])

            @block.gpsimd
            def _(pool):
                with pool.Fori(0, B) as b:
                    for n, unit in enumerate(UNITS):
                        c0 = first_query((HYP_G,) + unit)
                        pool.wait_ge(pvh_done, b * NU + n - 2 + 1 + TWO)
                        for half in range(2):
                            x = A[:, n % 2, 2 * half:2 * half + 2, c0:QT]
                            pool.wait_ge(taken, b * NHP + 2 * n + half + 1)
                            nc.gpsimd.tensor_tensor(EH[:, n % 2, 2 * half:2 * half + 2, c0:QT], x, x,
                                                    ALU.mult).then_inc(sq_done, 1)

            @block.vector
            def _(dve):
                v = nc.vector
                dve.sem_inc(os_ready, TWO)
                dve.sem_inc(side_free, TWO)
                for bank in obank:
                    v.memset(bank[:, :], 0.0).then_inc(banks_filled, 1)
                with dve.Fori(0, B) as b:
                    def least_a(qt, part):
                        n, m = (b * NQT + qt) * HYP_DVE, (b * NQT + qt) * HYP_ACT
                        j = slice(qt * JB, (qt + 1) * JB)
                        w0, w1 = hw[:, 0, j, :], hw[:, 1, j, :]
                        if part == 0:
                            v.tensor_scalar(w1, mhyp[:, j, :], ARG_MIN, None, ALU.max).then_inc(hyp_dve, 1)
                            dve.wait_ge(hyp_dve, n + 1)
                            v.tensor_tensor(w0, w1, w1, ALU.mult).then_inc(hyp_dve, 1)
                        elif part == 2:
                            dve.wait_ge(hyp_act, m + 2)
                            v.tensor_tensor(w1, w1, w0, ALU.add).then_inc(hyp_dve, 1)
                        elif part == 3:
                            dve.wait_ge(hyp_act, m + 3)
                            v.tensor_tensor(w1, w1, k["root"][:, :].unsqueeze(1).to_broadcast([P, JB, G]),
                                            ALU.mult).then_inc(hyp_dve, 1)
                            dve.wait_ge(hyp_dve, n + 4)
                            v.tensor_scalar(w1, w1, 1e-6, None, ALU.add).then_inc(hyp_dve, 1)

                    def take(n, half):
                        i, c0 = hyp_units[n], first_query((HYP_G,) + UNITS[n])
                        if n >= 2:
                            dve.wait_ge(sub_done, b * NHP + 2 * (n - 2) + half + 1)
                        dve.wait_ge(s_ready, b * 2 * NS + 2 * i + half + 1 + S0)
                        v.tensor_scalar(A[:, n % 2, 2 * half:2 * half + 2, c0:QT], score[half][:, :, c0:QT],
                                        ARG_MIN, None, ALU.max).then_inc(taken, 1)

                    def add_root(n, half):
                        dve.wait_ge(root_done, b * NHP + 2 * n + half + 1)
                        hh, c0 = slice(2 * half, 2 * half + 2), first_query((HYP_G,) + UNITS[n])
                        v.tensor_tensor(A[:, n % 2, hh, c0:QT], A[:, n % 2, hh, c0:QT], EH[:, n % 2, hh, c0:QT],
                                        ALU.add).then_inc(sum_done, 1)

                    def subtract(n, half):
                        unit = (HYP_G,) + UNITS[n]
                        hh, c0 = slice(2 * half, 2 * half + 2), first_query(unit)
                        if unit[2] == 0:
                            dve.wait_ge(side_free, b * NB + bank_of["spread", unit[1], G - 1] + 1 + TWO)
                        dve.wait_ge(rec_done, b * NHP + 2 * n + half + 1)
                        ins = v.tensor_tensor(EH[:, n % 2, hh, c0:QT], A[:, n % 2, hh, c0:QT], M[:, hh, c0:QT],
                                              ALU.subtract)
                        if on_diagonal(unit):
                            ins.then_inc(mask_step, 1)
                            dve.wait_ge(mask_step, b * NMASK + 2 * diag_hyp.index(n) + half + 1)
                            x = EH[:, n % 2, hh, c0:c0 + P]
                            ins = v.tensor_tensor(x, x, k["neg_up"][:, :].unsqueeze(1).to_broadcast([P, 2, P]),
                                                  ALU.add)
                        ins.then_inc(sub_done, 1)

                    def split(g, qt, before):
                        m = splits.index(("split", g, qt))
                        n = (b * len(splits) + m) * MSPLIT
                        nh = MAX_HEADS[g]


                        cols = mxp[:, :, :].rearrange("p (j h) c -> p j h c", h=G)[:, :, 0:nh, 0:qt + 1]
                        row = mrow[:, :].rearrange("p (j h) -> p j h", h=G)[:, :, 0:nh]
                        res = mres[:, :].rearrange("p (j h) -> p j h", h=G)[:, :, 0:nh]
                        part = mparts[:, m % 2, :, :].rearrange("p (j h) a -> p j h a", h=G)[:, :, 0:nh, :]
                        dve.wait_ge(side_free, b * NB + before + 1 + TWO)
                        v.tensor_reduce(row, cols, AX_X, ALU.max, negate=True).then_inc(split_step, 1)
                        dve.wait_ge(split_step, n + 1)
                        v.tensor_copy(part[:, :, :, 0], row).then_inc(split_step, 1)
                        dve.wait_ge(split_step, n + 2)
                        v.tensor_tensor(res, row, part[:, :, :, 0], ALU.subtract).then_inc(split_step, 1)
                        dve.wait_ge(split_step, n + 3)
                        v.tensor_copy(part[:, :, :, 1], res).then_inc(split_step, 1)
                        dve.wait_ge(split_step, n + 4)
                        v.tensor_tensor(part[:, :, :, 2], res, part[:, :, :, 1], ALU.subtract).then_inc(split_step, 1)

                    def side_task(task, before):
                        if task[0] == "split":
                            split(task[1], task[2], before)
                            return
                        n = bank_of[task]
                        src = sbank[n % 2]
                        dve.wait_ge(side_ready, b * NB + n + 1)
                        if task[0] == "chunk":
                            _, g, qt, j, c, h = task
                            wide = (j + 1) * P if c == qt else QT
                            v.tensor_reduce(mxp[:, j * G + h, c:c + 1], src[:, 0:wide], AX_X,
                                            ALU.min if g == HYP_G else ALU.max).then_inc(side_free, 1)
                            if g == HYP_G and (j, c, h) == (JB - 1, qt, G - 1):
                                dve.wait_ge(side_free, b * NB + n + 1 + TWO)
                                v.tensor_reduce(mhyp[:, qt * JB:(qt + 1) * JB, :].rearrange("p j h -> p (j h)"),
                                                mxp[:, :, 0:qt + 1], AX_X, ALU.min).then_inc(least_done, 1)
                                dve.wait_ge(least_done, b * NQT + qt + 1)
                        elif task[0] == "rows":
                            _, g, qt, hp = task
                            v.tensor_copy(QS[96:99, g, 2 * hp:2 * hp + 2, qt * QT:(qt + 1) * QT],
                                          src[:, :].bitcast(BF16)[96:99, :].rearrange("p (h t) -> p h t", h=2)
                                          ).then_inc(side_free, 1)
                        elif task[0] == "spread":
                            _, qt, h = task
                            if qt:
                                dve.wait_ge(sub_done, b * NHP + 2 * UNITS.index((qt, 0)))
                            v.tensor_copy(M[:, task[2], :], src[:, :]).then_inc(side_free, 1)
                        else:
                            tile = task[1]
                            o = src[:, :].rearrange("p (a w) -> p a w", w=32)
                            v.reciprocal(RZ[:, tile % 2, :], o[:, :, HD]).then_inc(rz_ready, 1)
                            dve.wait_ge(rz_ready, b * NTILE + tile + 1)
                            dve.wait_ge(y_stored[tile % 2], (b * (NTILE // 2) + tile // 2 + 1) * 16)
                            v.tensor_tensor(YT[:, tile % 2, :, :].rearrange("p j (h e) -> p (j h) e", e=HD),
                                            o[:, :, 0:HD], RZ[:, tile % 2, :].unsqueeze(2).to_broadcast(
                                                [P, JB * G, HD]), ALU.mult).then_inc(side_free, 1)

                    def evacuate(tile):
                        _, g, qt = ends[tile]
                        n = rank[g, qt, JB * (qt + 1) - 1]
                        if g == HYP_G:
                            dve.wait_ge(pvh_done, b * NU + n + 1 + TWO)
                        else:
                            dve.wait_ge(pv_done, b * len(PLAIN) + n + 1 + PV0)
                        v.tensor_copy(OS[:, tile % 2, :], obank[g == HYP_G][:, :]).then_inc(os_ready, 1)

                    before = -1
                    for i in range(NS + 3):
                        if i < NS and units[i][0] == HYP_G:
                            take(rank[units[i]], 0)
                            take(rank[units[i]], 1)
                        for tile, end in enumerate(ends):
                            if end[0] == i:
                                evacuate(tile)
                        for n in stage(i, "add"):
                            add_root(n, 0)
                            add_root(n, 1)
                        some = len(flow[i]) // 2
                        for task in flow[i][:some]:
                            side_task(task, before)
                            before = bank_of.get(task, before)
                        for n in stage(i, "subtract"):
                            subtract(n, 0)
                        for task in flow[i][some:]:
                            side_task(task, before)
                            before = bank_of.get(task, before)
                        for n in stage(i, "subtract"):
                            subtract(n, 1)
                        for qt in range(NQT):
                            least_a(qt, i - chain[qt])


def block_experts(nc, k, d):
    ctx = ExitStack()
    with ctx:
        def sb(name, shape, dt=F32):
            return ctx.enter_context(nc.sbuf_tensor("c_" + name, shape, dt))

        def ps(name):
            return ctx.enter_context(nc.psum_tensor("c_" + name, [P, 512], F32))

        def sem(name):
            return ctx.enter_context(nc.semaphore("c_" + name))

        CW = C + 1
        PAD = C + 8
        wproj = sb("wproj", [P, 2, C])
        pb, gamma, beta = sb("pb", [P, C]), sb("gamma", [P, C]), sb("beta", [P, C])
        mu = sb("mu", [P, 2, SLOTS])
        mu_sq = sb("mu_sq", [P, 2, SLOTS])
        mu_norm = sb("mu_norm", [P, SLOTS])
        scale = sb("scale", [P, 1])
        ones = sb("ones", [P, P])
        w1 = sb("w1", [P, 2, E, HID])
        b1T = sb("b1T", [HID, E])
        w2 = sb("w2", [HID, E, C])
        b2r = sb("b2r", [P, 2, C])
        Y = sb("Y", [P, NT, C])
        X = sb("X", [P, NT, C])
        X2 = sb("X2", [P, NT, C])
        L = sb("L", [P, NT, C])
        XN = sb("XN", [P, NT, PAD])
        EC = sb("EC", [P, NT, SLOTS])
        ECT = sb("ECT", [P, 2, T])
        D = sb("D", [P, NT, SLOTS])
        yT = sb("yT", [P, U, 2, P])
        N_ = sb("normed", [P, U, C])
        stats = sb("stats", [P, NT, 6])
        st = sb("st", [P, 6, NT])
        hn = sb("hn", [P, 4, NT])
        nmax = sb("nmax", [P, NT])
        cmax = sb("cmax", [P, SLOTS])
        cmaxT = sb("cmaxT", [P, 2])
        rz = sb("rz", [P, 2])
        rzo = sb("rzo", [P, NT])
        SI = sb("SI", [P, 2, C])
        SIT = sb("SIT", [P, 2, SLOTS])
        HT = sb("HT", [HID, SLOTS])
        HG = sb("HG", [HID, SLOTS])
        SOT = sb("SOT", [P, 2, SLOTS])
        SO = sb("SO", [P, 2, PAD])

        tp_bank = [ps(f"tp{u}") for u in range(2)]
        mm_bank = [ps(f"mm{u}") for u in range(2)]
        et_bank = [ps(f"et{u}") for u in range(2)]
        si_bank = [ps(f"si{u}") for u in range(2)]
        tp_half, mm_half, et_half = ([bank[u // 2][:, u % 2 * C:(u % 2 + 1) * C] for u in range(U)]
                                     for bank in (tp_bank, mm_bank, et_bank))
        fo_bank = mm_bank + tp_bank

        (weights, filled, prep, mu_psum, mu_root, x_loaded, y_loaded, out_stored) = map(
            sem, ["weights", "filled", "prep", "mu_psum", "mu_root", "x_loaded", "y_loaded", "out_stored"])
        (yt_psum, yt_ready, ao_psum, ao_ready, bs_done, var_ready, std_ready, rstd_ready) = map(
            sem, ["yt_psum", "yt_ready", "ao_psum", "ao_ready", "bs_done", "var_ready", "std_ready", "rstd_ready"])
        (n_ready, x2_ready, hn_step, hn_root, len_root, xn_a, xn_b, xn_ready) = map(
            sem, ["n_ready", "x2_ready", "hn_step", "hn_root", "len_root", "xn_a", "xn_b", "xn_ready"])
        (xnt_psum, xnt_ready, l_psum, l_ready, nmax_ready, ec_ready, ect_psum, ect_ready) = map(
            sem, ["xnt_psum", "xnt_ready", "l_psum", "l_ready", "nmax_ready", "ec_ready", "ect_psum", "ect_ready"])
        (cmax_ready, cmaxT_psum, cmaxT_ready, cmb_psum, d_sub, d_ready, si_psum, si_step) = map(
            sem, ["cmax_ready", "cmaxT_psum", "cmaxT_ready", "cmb_psum", "d_sub", "d_ready", "si_psum", "si_step"])
        (sit_psum, sit_ready, h_psum, h_ready, hg_ready, sot_psum, sot_ready, so_psum, so_ready) = map(
            sem, ["sit_psum", "sit_ready", "h_psum", "h_ready", "hg_ready", "sot_psum", "sot_ready", "so_psum",
                  "so_ready"])
        (fo_psum, fo_step, fo_ready, n2_ready, out_ready) = map(
            sem, ["fo_psum", "fo_step", "fo_ready", "n2_ready", "out_ready"])

        storing = sem("storing")
        NW = 10 + E
        HNS = 11
        DC = 4
        ND = NT // DC

        def col(buf, n):
            return buf[:, bass.ds(n, 1), 0:C].rearrange("p o c -> p (o c)")

        with nc.Block() as block:
            @block.sync
            def _(sp):
                def load_y(b, first):
                    sp.dma_start(Y[:, :, :], d["y_dram"][first:, :, :][bass.ds(b, 1), :, :].rearrange(
                        "o (n p) c -> p (o n) c", p=P)).then_inc(y_loaded, 16)

                def load_x(b, first):
                    sp.dma_start(X[:, :, :], d["x"][first:, :, :][bass.ds(b, 1), :, :].rearrange(
                        "o (n p) c -> p (o n) c", p=P)).then_inc(x_loaded, 16)

                load_y(0, 0)
                for dst, src in [(wproj[:, :, :], d["wproj"].rearrange("(k p) n -> p k n", p=P)),
                                 (pb[:, :], d["pb"].partition_broadcast(P)),
                                 (mu[:, :, :], d["mu"].rearrange("(k p) e s -> p k (e s)", p=P)),
                                 (gamma[:, :], d["gamma"].partition_broadcast(P)),
                                 (beta[:, :], d["beta"].partition_broadcast(P)),
                                 (scale[:, :], d["scale"].partition_broadcast(P)),
                                 (w1[:, 0, :, :], d["w1"][:, 0:P, :].rearrange("e p h -> p e h")),
                                 (w1[:, 1, :, :], d["w1"][:, P:C, :].rearrange("e p h -> p e h")),
                                 (b1T[:, :], d["b1T"]),
                                 (w2[:, :, :], d["w2"].rearrange("e h c -> h e c"))]:
                    sp.dma_start(dst, src).then_inc(weights, 16)
                for e in range(E):
                    sp.dma_start(b2r[e % 8 * S:(e % 8 + 1) * S, e // 8, :],
                                 d["b2"][e, :].partition_broadcast(S)).then_inc(weights, 16)
                load_x(0, 0)

                def store(b):
                    for m in range(ND):
                        sp.wait_ge(out_ready, b * NT + (m + 1) * DC + U)
                        if m == 0:
                            sp.sem_inc(storing, 1)
                        sp.dma_start(d["out"][bass.ds(b, 1), m * DC * P:(m + 1) * DC * P, :].rearrange(
                            "o (n p) c -> p (o n) c", p=P), X2[:, m * DC:(m + 1) * DC, :]).then_inc(out_stored, 16)

                with sp.Fori(0, B - 1) as b:
                    sp.wait_ge(yt_psum, b * NT + NT)
                    load_y(b, 1)
                    sp.wait_ge(x2_ready, b * NT + NT + U)
                    load_x(b, 1)
                    store(b)
                store(B - 1)
                sp.wait_ge(out_stored, 16 * ND * (B + 1))

            @block.gpsimd
            def _(pool):
                g = nc.gpsimd
                pool.sem_inc(out_stored, 16 * ND)
                g.memset(ones[:, :], 1.0).then_inc(filled, 1)
                g.memset(XN[:, :, C:CW], 1.0).then_inc(filled, 1)
                g.memset(SO[:, :, C:CW], 1.0).then_inc(filled, 1)
                pool.wait_ge(weights, 16 * NW)
                with pool.Fori(0, B) as b:
                    with pool.Fori(0, NT // U) as m:
                        for u in range(U):
                            i = b * NT + m * U + u
                            n = m * U + u
                            pool.wait_ge(xn_b, i + 1)
                            g.tensor_tensor(col(XN, n), col(XN, n), beta[:, :], ALU.add).then_inc(xn_ready, 1)

            @block.vector
            def _(dve):
                v = nc.vector
                dve.sem_inc(ao_ready, U)
                dve.sem_inc(x2_ready, U)
                dve.sem_inc(l_ready, U)
                dve.sem_inc(fo_ready, U)
                dve.sem_inc(out_ready, U)
                dve.sem_inc(so_ready, 1)
                dve.wait_ge(weights, 16 * NW)
                dve.wait_ge(filled, 3)
                v.tensor_tensor(mu_sq[:, :, :], mu[:, :, :], mu[:, :, :], ALU.mult).then_inc(prep, 1)
                dve.wait_ge(mu_root, 1)
                v.tensor_scalar(mu_norm[:, :], mu_norm[:, :], 1e-12, None, ALU.max).then_inc(prep, 1)
                dve.wait_ge(prep, 2)
                v.reciprocal(mu_norm[:, :], mu_norm[:, :]).then_inc(prep, 1)
                dve.wait_ge(prep, 3)
                v.tensor_tensor(mu[:, :, :], mu[:, :, :], mu_norm[:, :].unsqueeze(1).to_broadcast([P, 2, SLOTS]),
                                ALU.mult).then_inc(prep, 1)

                with dve.Fori(0, B) as b:
                    steps = [0]

                    def step(ins):
                        steps[0] += 1
                        ins.then_inc(hn_step, 1)
                        dve.wait_ge(hn_step, b * HNS + steps[0])

                    with dve.Fori(0, NT // U) as m:
                        for u in range(U):
                            i, n = b * NT + m * U + u, m * U + u
                            dve.wait_ge(ao_psum, i + 1 - u + (u | 1) + U)
                            v.tensor_tensor(col(L, n), mm_half[u], pb[:, :], ALU.add).then_inc(ao_ready, 1)
                        for u in range(U):
                            i, n = b * NT + m * U + u, m * U + u
                            dve.wait_ge(ao_ready, i + 1 + U)
                            v.bn_stats(stats[:, bass.ds(n, 1), :].rearrange(
                                "p o s -> p (o s)"), col(L, n)).then_inc(bs_done, 1)
                    dve.wait_ge(bs_done, b * 4 * NT + NT)
                    layer_norm_stats(nc, dve, stats, st, b * 3, var_ready, std_ready, rstd_ready)
                    with dve.Fori(0, NT // U) as m:
                        dve.wait_ge(x_loaded, b * 16 + 16)
                        dve.wait_ge(out_stored, (b + 1) * 16 * ND)
                        for u in range(U):
                            i, n = b * NT + m * U + u, m * U + u
                            dve.wait_ge(n_ready, i + 1)
                            v.tensor_tensor(col(X2, n), col(X, n), N_[:, u, :], ALU.add).then_inc(x2_ready, 1)
                        for u in range(U):
                            i, n = b * NT + m * U + u, m * U + u
                            dve.wait_ge(x2_ready, i + 1 + U)
                            v.bn_stats(stats[:, bass.ds(n, 1), :].rearrange("p o s -> p (o s)"),
                                       col(X2, n)).then_inc(bs_done, 1)
                    dve.wait_ge(bs_done, b * 4 * NT + 2 * NT)
                    layer_norm_stats(nc, dve, stats, st, b * 3 + 1, var_ready, std_ready, rstd_ready)
                    dve.wait_ge(rstd_ready, (b * 3 + 2) * 2)
                    step(v.tensor_tensor(hn[:, 0, :], st[:, 3, :], st[:, 5, :], ALU.mult))
                    step(v.tensor_tensor(hn[:, 0, :], hn[:, 0, :], st[:, 5, :], ALU.mult))
                    dve.wait_ge(hn_root, b + 1)
                    step(v.reciprocal(hn[:, 2, :], hn[:, 1, :]))
                    step(v.tensor_tensor(hn[:, 3, :], st[:, 0, :], hn[:, 2, :], ALU.mult))
                    steps[0] += 1
                    v.tensor_tensor(hn[:, 2, :], st[:, 5, :], hn[:, 2, :], ALU.mult).then_inc(hn_step, 1)
                    with dve.Fori(0, NT // U) as m:
                        for u in range(U):
                            i, n = b * NT + m * U + u, m * U + u
                            dve.wait_ge(xn_a, i + 1)
                            v.tensor_tensor(col(XN, n), col(XN, n), gamma[:, :], ALU.mult).then_inc(xn_b, 1)
                        for u in range(U):
                            i, n = b * NT + m * U + u, m * U + u
                            dve.wait_ge(xn_ready, i + 1)
                            v.bn_stats(stats[:, bass.ds(n, 1), :].rearrange("p o s -> p (o s)"),
                                       col(XN, n)).then_inc(bs_done, 1)
                    dve.wait_ge(bs_done, b * 4 * NT + 3 * NT)
                    pick = stats[:, :, :].rearrange("p n s -> p s n")
                    step(v.tensor_tensor(st[:, 0, :], pick[:, 1, :], pick[:, 1, :], ALU.mult))
                    step(v.tensor_tensor(st[:, 1, :], pick[:, 4, :], pick[:, 4, :], ALU.mult))
                    step(v.tensor_tensor(st[:, 0, :], st[:, 0, :], st[:, 1, :], ALU.add))
                    step(v.tensor_tensor(st[:, 1, :], pick[:, 2, :], pick[:, 5, :], ALU.add))
                    step(v.scalar_tensor_tensor(out=hn[:, 0, :], in0=st[:, 0, :], scalar=C / 2.0, in1=st[:, 1, :],
                                                op0=ALU.mult, op1=ALU.add))
                    dve.wait_ge(len_root, b + 1)
                    step(v.tensor_scalar(hn[:, 1, :], hn[:, 1, :], 1e-12, None, ALU.max))
                    v.reciprocal(hn[:, 0, :], hn[:, 1, :]).then_inc(prep, 1)
                    dve.wait_ge(prep, 4 + b * 2 + 1)
                    v.tensor_scalar(hn[:, 0, :], hn[:, 0, :], scale[:, :], None, ALU.mult).then_inc(prep, 1)
                    with dve.Fori(0, NT // U) as m:
                        dve.wait_ge(prep, 4 + b * 2 + 2)
                        assert steps[0] == HNS
                        for u in range(U):
                            i, n = b * NT + m * U + u, m * U + u
                            dve.wait_ge(l_psum, i + 1 - u + (u | 1) + U)
                            v.tensor_scalar(col(L, n), mm_half[u], hn[:, 0, bass.ds(n, 1)], None,
                                            ALU.mult).then_inc(l_ready, 1)
                        for u in range(U):
                            i, n = b * NT + m * U + u, m * U + u
                            dve.wait_ge(l_ready, i + 1 + U)
                            v.tensor_reduce(nmax[:, bass.ds(n, 1)], col(L, n), AX_X, ALU.max,
                                            negate=True).then_inc(nmax_ready, 1)
                    v.tensor_reduce(cmax[:, :], L[:, :, :].rearrange("p n s -> p s n"), AX_X,
                                    ALU.max).then_inc(cmax_ready, 1)
                    dve.wait_ge(cmaxT_psum, b + 1)
                    v.tensor_reduce(cmaxT[:, :], si_bank[0][:, 0:2 * P].rearrange("p (c t) -> p c t", c=2), AX_X,
                                    ALU.max).then_inc(cmaxT_ready, 1)
                    dve.wait_ge(cmb_psum, b + 1)
                    for m in range(ND):
                        t_ = slice(m * DC, (m + 1) * DC)
                        v.tensor_tensor(D[:, t_, :], L[:, t_, :], si_bank[1][:, 0:SLOTS].unsqueeze(1).to_broadcast(
                            [P, DC, SLOTS]), ALU.subtract).then_inc(d_sub, 1)
                    dve.wait_ge(si_psum, b + 1)
                    for c in range(2):
                        v.reciprocal(rz[:, c:c + 1], si_bank[c][:, C:CW]).then_inc(si_step, 1)
                    for c in range(2):
                        dve.wait_ge(si_step, b * 4 + c + 1)
                        v.tensor_scalar(SI[:, c, :], si_bank[c][:, 0:C], rz[:, c:c + 1], None,
                                        ALU.mult).then_inc(si_step, 1)
                    dve.wait_ge(sit_psum, b + 1)
                    v.tensor_copy(SIT[:, :, :].rearrange("p k s -> p (k s)"), et_bank[0][:, :]).then_inc(sit_ready, 1)
                    dve.wait_ge(h_psum, b + 1)
                    v.tensor_tensor(HT[:, :].rearrange("h (e s) -> h e s", s=S),
                                    et_bank[1][0:HID, 0:SLOTS].rearrange("h (e s) -> h e s", s=S),
                                    b1T[:, :].unsqueeze(2).to_broadcast([HID, E, S]), ALU.add).then_inc(h_ready, 1)
                    dve.wait_ge(sot_psum, b + 1)
                    v.tensor_copy(SOT[:, :, :].rearrange("p k s -> p (k s)"), et_bank[0][:, :]).then_inc(sot_ready, 1)
                    dve.wait_ge(so_psum, b + 1)
                    v.tensor_tensor(SO[:, :, 0:C], et_bank[1][:, :].rearrange("p (c d) -> p c d", c=2), b2r[:, :, :],
                                    ALU.add).then_inc(so_ready, 1)
                    with dve.Fori(0, NT // U) as m:
                        for u in range(U):
                            i, n = b * NT + m * U + u, m * U + u
                            dve.wait_ge(fo_psum, i + 1)
                            v.reciprocal(rzo[:, bass.ds(n, 1)], fo_bank[u][:, C:CW]).then_inc(fo_step, 1)
                        for u in range(U):
                            i, n = b * NT + m * U + u, m * U + u
                            dve.wait_ge(fo_step, i + 1)
                            v.tensor_scalar(col(L, n), fo_bank[u][:, 0:C], rzo[:, bass.ds(n, 1)], None,
                                            ALU.mult).then_inc(fo_ready, 1)
                        for u in range(U):
                            i, n = b * NT + m * U + u, m * U + u
                            dve.wait_ge(fo_ready, i + 1 + U)
                            v.bn_stats(stats[:, bass.ds(n, 1), :].rearrange("p o s -> p (o s)"),
                                       col(L, n)).then_inc(bs_done, 1)
                    dve.wait_ge(bs_done, b * 4 * NT + 4 * NT)
                    layer_norm_stats(nc, dve, stats, st, b * 3 + 2, var_ready, std_ready, rstd_ready)
                    with dve.Fori(0, NT // U) as m:
                        for u in range(U):
                            i, n = b * NT + m * U + u, m * U + u
                            dve.wait_ge(n2_ready, i + 1)
                            v.tensor_tensor(col(X2, n), col(X2, n), N_[:, u, :], ALU.add).then_inc(out_ready, 1)

            @block.scalar
            def _(act):
                a = nc.scalar
                act.sem_inc(yt_ready, U)
                act.sem_inc(xnt_ready, U)
                act.sem_inc(ect_ready, U)
                act.wait_ge(mu_psum, 1)
                a.activation(mu_norm[:, :], si_bank[0][:, 0:SLOTS], ACT.Sqrt).then_inc(mu_root, 1)

                def root_of_variance(r):
                    act.wait_ge(var_ready, r * VAR + VAR)
                    a.activation(st[:, 4, :], st[:, 3, :], ACT.Sqrt, bias=k["eps_ln"][:, :],
                                 scale=1.0 / C).then_inc(std_ready, 1)
                    act.wait_ge(rstd_ready, r * 2 + 2)

                with act.Fori(0, B) as b:
                    with act.Fori(0, NT // U) as m:
                        for u in range(U):
                            i = b * NT + m * U + u
                            act.wait_ge(yt_psum, i + 1 - u + (u | 1))
                            act.wait_ge(ao_psum, i + 1)
                            a.copy(yT[:, u, :, :].rearrange("p k t -> p (k t)"),
                                   tp_half[u]).then_inc(yt_ready, 1)
                    root_of_variance(b * 3)
                    with act.Fori(0, NT // U) as m:
                        for u in range(U):
                            i, n = b * NT + m * U + u, m * U + u
                            act.wait_ge(x2_ready, i + 1)
                            a.activation(N_[:, u, :], col(L, n), ACT.Identity, bias=st[:, 0, bass.ds(n, 1)],
                                         scale=st[:, 5, bass.ds(n, 1)]).then_inc(n_ready, 1)
                    root_of_variance(b * 3 + 1)
                    act.wait_ge(hn_step, b * HNS + 2)
                    a.activation(hn[:, 1, :], hn[:, 0, :], ACT.Sqrt, bias=k["eps_ln"][:, :],
                                 scale=1.0 / C).then_inc(hn_root, 1)
                    act.wait_ge(hn_step, b * HNS + 5)
                    with act.Fori(0, NT // U) as m:
                        for u in range(U):
                            i, n = b * NT + m * U + u, m * U + u
                            a.activation(col(XN, n), col(X2, n), ACT.Identity, bias=hn[:, 3, bass.ds(n, 1)],
                                         scale=hn[:, 2, bass.ds(n, 1)]).then_inc(xn_a, 1)
                    act.wait_ge(hn_step, b * HNS + 10)
                    a.activation(hn[:, 1, :], hn[:, 0, :], ACT.Sqrt).then_inc(len_root, 1)
                    def copy_xn(m):
                        for u in range(U):
                            i = b * NT + m * U + u
                            act.wait_ge(xnt_psum, i + 1 - u + (u | 1))
                            act.wait_ge(l_psum, i + 1)
                            a.copy(yT[:, u, :, :].rearrange("p k t -> p (k t)"),
                                   tp_half[u]).then_inc(xnt_ready, 1)

                    def combine_exp(m):
                        for u in range(U):
                            i, n = b * NT + m * U + u, m * U + u
                            act.wait_ge(nmax_ready, i + 1)
                            a.activation(col(EC, n), col(L, n), ACT.Exp,
                                         bias=nmax[:, bass.ds(n, 1)]).then_inc(ec_ready, 1)
                        for u in range(U):
                            i, n = b * NT + m * U + u, m * U + u
                            act.wait_ge(ect_psum, i + 1 - u + (u | 1))
                            a.copy(ECT[:, :, bass.ds(m * U * P + u * P, P)],
                                   et_half[u].rearrange("p (c t) -> p c t", c=2)).then_inc(ect_ready, 1)

                    a.preload_act_table_set("exp_and_others")
                    copy_xn(0)
                    copy_xn(1)
                    with act.Fori(0, NT // U - 2) as m:
                        combine_exp(m)
                        copy_xn(m + 2)
                    for m in range(NT // U - 2, NT // U):
                        combine_exp(m)
                    for m in range(ND):
                        act.wait_ge(d_sub, b * ND + m + 1)
                        x = D[:, m * DC:(m + 1) * DC, :]
                        a.activation(x, x, ACT.Exp).then_inc(d_ready, 1)
                    act.wait_ge(h_ready, b + 1)
                    a.activation(HG[:, :], HT[:, :], ACT.Gelu).then_inc(hg_ready, 1)
                    root_of_variance(b * 3 + 2)
                    with act.Fori(0, NT // U) as m:
                        for u in range(U):
                            i, n = b * NT + m * U + u, m * U + u
                            act.wait_ge(out_ready, i + 1)
                            a.activation(N_[:, u, :], col(L, n), ACT.Identity, bias=st[:, 0, bass.ds(n, 1)],
                                         scale=st[:, 5, bass.ds(n, 1)]).then_inc(n2_ready, 1)

            @block.tensor
            def _(pe):
                t = nc.tensor
                pe.sem_inc(ao_psum, U)
                pe.sem_inc(l_psum, U)
                pe.wait_ge(prep, 1)
                for c in range(2):
                    ins = t.matmul(si_bank[0][:, 0:SLOTS], ones[:, :], mu_sq[:, c, :], start=(c == 0), stop=(c == 1))
                ins.then_inc(mu_psum, 1)
                pe.wait_ge(mu_root, 1)
                with pe.Fori(0, B) as b:
                    def product(out, lhs, rhs):
                        for c in range(2):
                            ins = t.matmul(out, lhs(c), rhs(c), start=(c == 0), stop=(c == 1))
                        return ins

                    def turn(out, src):
                        for c in range(2):
                            ins = t.transpose(out[:, c * P:(c + 1) * P], src[:, c * P:(c + 1) * P], k["ident"][:, :])
                        return ins

                    pe.wait_ge(y_loaded, b * 16 + 16)
                    pe.wait_ge(xnt_ready, b * NT + U)
                    pe.wait_ge(fo_ready, b * NT + U)
                    for n in range(NT + 2):
                        if n < NT:
                            pe.wait_ge(yt_ready, b * NT + (n | 1) + 1)
                            turn(tp_half[n % U], Y[:, n, :]).then_inc(yt_psum, 1)
                        if n >= 2:
                            j = n - 2
                            pe.wait_ge(yt_ready, b * NT + j + 1 + U)
                            pe.wait_ge(ao_ready, b * NT + (j | 1) + 1)
                            product(mm_half[j % U], lambda c: yT[:, j % U, c, :],
                                    lambda c: wproj[:, c, :]).then_inc(ao_psum, 1)
                    pe.wait_ge(ao_ready, b * NT + NT + U)

                    def turn_xn(m):
                        for n in range(U * m, U * m + U):
                            pe.wait_ge(xn_ready, b * NT + n + 1)
                            pe.wait_ge(xnt_ready, b * NT + (n | 1) + 1)
                            turn(tp_half[n % U], XN[:, n, :]).then_inc(xnt_psum, 1)

                    def logits(m):
                        for n in range(U * m, U * m + U):
                            pe.wait_ge(xnt_ready, b * NT + n + 1 + U)
                            pe.wait_ge(l_ready, b * NT + (n | 1) + 1)
                            product(mm_half[n % U], lambda c: yT[:, n % U, c, :],
                                    lambda c: mu[:, c, :]).then_inc(l_psum, 1)

                    turn_xn(0)
                    logits(0)
                    turn_xn(1)
                    for m in range(NT // U):
                        if m + 1 < NT // U:
                            logits(m + 1)
                        for n in range(U * m, U * m + U):
                            if n == 0:
                                pe.wait_ge(so_ready, b + 1)
                            pe.wait_ge(ec_ready, b * NT + n + 1)
                            pe.wait_ge(ect_ready, b * NT + (n | 1) + 1)
                            turn(et_half[n % U], EC[:, n, :]).then_inc(ect_psum, 1)
                        if m + 2 < NT // U:
                            turn_xn(m + 2)
                    pe.wait_ge(cmax_ready, b + 1)
                    turn(si_bank[0], cmax[:, :]).then_inc(cmaxT_psum, 1)
                    pe.wait_ge(cmaxT_ready, b + 1)
                    for c in range(2):
                        ins = t.matmul(si_bank[1][:, c * P:(c + 1) * P], cmaxT[:, c:c + 1].to_broadcast([P, P]),
                                       k["ident"][:, :], start=True, stop=True)
                    ins.then_inc(cmb_psum, 1)
                    for n in range(NT):
                        if n % DC == 0:
                            pe.wait_ge(d_ready, b * ND + n // DC + 1)
                        if n == 0:
                            pe.wait_ge(d_sub, b * ND + ND)
                        for c in range(2):
                            ins = t.matmul(si_bank[c][:, 0:CW], D[:, n, c * P:(c + 1) * P], XN[:, n, 0:CW],
                                           start=(n == 0), stop=(n == NT - 1))
                    ins.then_inc(si_psum, 1)
                    pe.wait_ge(ect_ready, b * NT + NT + U)
                    pe.wait_ge(si_step, b * 4 + 4)
                    for kk in range(2):
                        for c in range(2):
                            ins = t.transpose(et_bank[0][:, (kk * 2 + c) * P:(kk * 2 + c + 1) * P],
                                              SI[:, c, kk * P:(kk + 1) * P], k["ident"][:, :])
                    ins.then_inc(sit_psum, 1)
                    pe.wait_ge(sit_ready, b + 1)
                    for e in range(E):
                        ins = product(et_bank[1][0:HID, e * S:(e + 1) * S], lambda c: w1[:, c, e, :],
                                      lambda c: SIT[:, c, e * S:(e + 1) * S])
                    ins.then_inc(h_psum, 1)
                    pe.wait_ge(hg_ready, b + 1)
                    for e in range(E):
                        for kk in range(2):
                            ins = t.matmul(et_bank[0][:, kk * SLOTS + e * S:kk * SLOTS + (e + 1) * S],
                                           w2[:, e, kk * P:(kk + 1) * P], HG[:, e * S:(e + 1) * S], start=True,
                                           stop=True)
                    ins.then_inc(sot_psum, 1)
                    pe.wait_ge(sot_ready, b + 1)
                    for c in range(2):
                        for kk in range(2):
                            ins = t.transpose(et_bank[1][:, (c * 2 + kk) * P:(c * 2 + kk + 1) * P],
                                              SOT[:, kk, c * P:(c + 1) * P], k["ident"][:, :])
                    ins.then_inc(so_psum, 1)
                    pe.wait_ge(so_ready, b + 2)
                    pe.wait_ge(l_ready, b * NT + NT + U)
                    for n in range(NT):
                        pe.wait_ge(fo_ready, b * NT + n + 1)
                        product(fo_bank[n % U][:, 0:CW], lambda c: ECT[:, c, n * P:(n + 1) * P],
                                lambda c: SO[:, c, 0:CW]).then_inc(fo_psum, 1)


HEADS = [*range(N_STD), *range(N_STD + N_HYP, H), *range(N_STD, N_STD + N_HYP)]


def build(nc, **d):
    with ExitStack() as ctx:
        d["parts"] = nc.dram_tensor("parts", (B, 2, H // 2, 2 * HW3, T), BF16, kind="Internal").ap()
        d["parts_h"] = d["parts"].rearrange("b q a (x r) t -> b q (a x) r t", x=2)
        d["v_dram"] = nc.dram_tensor("v_dram", (B, NG, P, NT, G * PW), F32, kind="Internal").ap()
        d["y_dram"] = nc.dram_tensor("y_dram", (B, T, C), F32, kind="Internal").ap()
        k = build_constants(nc, ctx, d)
        block_constants(nc, ctx, k, d)
        block_project(nc, k, d)
        block_attend(nc, k, d)
        block_experts(nc, k, d)


def kernel(**inputs):
    import numpy as np
    import concourse.bacc as bacc
    from concourse.bass_utils import run_bass_kernel_spmd

    x = np.ascontiguousarray(inputs["L0_attn_x"])
    frequency = 1.0 / 10000.0 ** (np.arange(0, HD, 2, dtype=np.float32) / np.float32(HD))
    angle = np.outer(np.arange(T, dtype=np.float32), frequency.astype(np.float32)).astype(np.float32)
    arrays = {
        "x": x,
        "wqkv": inputs["L0_attn_qkv_w"].reshape(3, H, HD, C)[:, HEADS].reshape(3 * C, C).T,
        "wproj": inputs["L0_attn_proj_w"].reshape(C, H, HD)[:, HEADS].reshape(C, C).T,
        "pb": inputs["L0_attn_proj_b"],
        "curv": inputs["L0_attn_curvature"].reshape(N_HYP),
        "cos": np.cos(angle),
        "sin": np.sin(angle),
        "gamma": inputs["L0_ffn_ln_gamma"],
        "beta": inputs["L0_ffn_ln_beta"],
        "mu": inputs["L0_ffn_mu"],
        "scale": inputs["L0_ffn_scale"],
        "w1": inputs["L0_ffn_w1"],
        "b1T": inputs["L0_ffn_b1"].T,
        "w2": inputs["L0_ffn_w2"],
        "b2": inputs["L0_ffn_b2"],
    }
    arrays = {name: np.ascontiguousarray(a) for name, a in arrays.items()}
    nc = bacc.Bacc("TRN2", target_bir_lowering=False, num_devices=1)
    args = {name: nc.dram_tensor(name, a.shape, mybir.dt.from_np(a.dtype), kind="ExternalInput").ap()
            for name, a in arrays.items()}
    args["out"] = nc.dram_tensor("out", (B, T, C), F32, kind="ExternalOutput").ap()
    build(nc, **args)
    r = run_bass_kernel_spmd(nc, [arrays], core_ids=[0])
    return r.results[0]["out"]
```
